# Optimizing a Trainium2 kernel written in Bass

```python
import numpy as np
import jax
import jax.numpy as jnp

def _softmax(x, axis=-1):
    return jax.nn.softmax(x, axis=axis)

def _gelu(x):
    return jax.nn.gelu(x, approximate=True)

def _silu(x):
    return jax.nn.silu(x)

def _sigmoid(x):
    return jax.nn.sigmoid(x)

def _layernorm(x, axis=-1, eps=1e-05):
    m = jnp.mean(x, axis=axis, keepdims=True)
    v = jnp.var(x, axis=axis, keepdims=True)
    return (x - m) / jnp.sqrt(v + eps)

def _scatter_add(tgt, idx, src, axis=0):
    return tgt.at[idx].add(src)

def _segment_sum(src, seg, n):
    return jax.ops.segment_sum(src, seg, n)
kernel_name = 'mk_gnn_ffn_d1_gnn_r8_1a490a'

def setup_inputs(seed: int=0):
    np.random.seed(seed)
    _w = jnp.asarray

    def _rec_inputs():
        import jax
        import jax.numpy as jnp
        _gk = jax.random.key(seed)
        x = -0.0003713 + 1 * jax.random.normal(jax.random.fold_in(_gk, 1), (6250, 256), jnp.float32)
        src = jax.random.randint(jax.random.fold_in(_gk, 2), (100000,), 0, 6250, jnp.int32)
        dst = jax.random.randint(jax.random.fold_in(_gk, 3), (100000,), 0, 6250, jnp.int32)
        _o = jnp.argsort(dst, stable=True)
        src = src[_o]
        dst = dst[_o]
        return (x, src, dst)
    x, src, dst = _rec_inputs()

    def _L0_gnn_setup():
        import jax, jax.numpy as jnp
        import numpy as np
        N, E = (6250, 100000)
        IN_DIM, HEADS, OUT_DIM = (256, 8, 32)
        NEG_SLOPE = 0.2
        LN_EPS = 1e-05
        key = jax.random.key(seed)
        ks = jax.random.split(key, 8)
        HC = HEADS * OUT_DIM
        x = jax.random.normal(ks[0], (N, IN_DIM), dtype=jnp.float32)
        edge_index = jax.random.randint(ks[1], (2, E), 0, N, dtype=jnp.int32)
        W = jax.random.normal(ks[2], (IN_DIM, HC), dtype=jnp.float32) / np.sqrt(IN_DIM)
        att_src = jax.random.normal(ks[3], (HEADS, OUT_DIM), dtype=jnp.float32) / np.sqrt(OUT_DIM)
        att_dst = jax.random.normal(ks[4], (HEADS, OUT_DIM), dtype=jnp.float32) / np.sqrt(OUT_DIM)
        bias = jnp.zeros((HC,), dtype=jnp.float32)
        ln_gamma = jnp.ones((HC,), dtype=jnp.float32)
        ln_beta = jnp.zeros((HC,), dtype=jnp.float32)
        return {'x': x, 'edge_index': edge_index, 'W': W, 'att_src': att_src, 'att_dst': att_dst, 'bias': bias, 'ln_gamma': ln_gamma, 'ln_beta': ln_beta}
    _L0_gnn_all = _L0_gnn_setup()
    _L0_gnn_in = {k: v for k, v in _L0_gnn_all.items() if k in ('W', 'att_src', 'att_dst', 'bias', 'ln_gamma', 'ln_beta')}
    del _L0_gnn_all

    def _L0_ffn_setup():
        import jax, jax.numpy as jnp
        import numpy as np
        B, N, D = (16, 512, 256)
        NUM_EXPERTS, TOP_K, HEADS = (4, 2, 4)
        N_EDGES = 131072
        LN_EPS = 1e-05

        def _layernorm(x, g, b):
            mu = x.mean(-1, keepdims=True)
            var = ((x - mu) ** 2).mean(-1, keepdims=True)
            return (x - mu) * jax.lax.rsqrt(var + LN_EPS) * g + b

        def _forward(x, edge_index, W_gat, att_src, att_dst, b_gat, ln_gamma, ln_beta, W1, b1, W2, b2):
            Bc, Nc, Dc = x.shape
            M = Bc * Nc
            x_flat = x.reshape(M, Dc)
            h = (x_flat @ W_gat).reshape(M, HEADS, NUM_EXPERTS)
            loops = jnp.arange(M, dtype=edge_index.dtype)
            src = jnp.concatenate([edge_index[0], loops])
            dst = jnp.concatenate([edge_index[1], loops])
            a_src = (h * att_src).sum(-1)
            a_dst = (h * att_dst).sum(-1)
            e = jax.nn.leaky_relu(a_src[src] + a_dst[dst], negative_slope=0.2)
            e_max = jax.ops.segment_max(e, dst, num_segments=M)
            ee = jnp.exp(e - e_max[dst])
            denom = jax.ops.segment_sum(ee, dst, num_segments=M)
            alpha = ee / (denom[dst] + 1e-16)
            msg = h[src] * alpha[:, :, None]
            agg = jax.ops.segment_sum(msg, dst, num_segments=M).reshape(M, HEADS * NUM_EXPERTS) + b_gat
            scores = _layernorm(agg, ln_gamma, ln_beta).reshape(M, HEADS, NUM_EXPERTS).mean(1)
            scores = scores.reshape(Bc, Nc, NUM_EXPERTS)
            topk_s, topk_i = jax.lax.top_k(scores, TOP_K)
            w = jax.nn.softmax(topk_s, axis=-1)
            out = jnp.zeros_like(x)
            for ei in range(NUM_EXPERTS):
                g = jnp.where(topk_i == ei, w, 0.0).sum(-1)
                hh = jax.nn.gelu(x @ W1[ei] + b1[ei], approximate=False)
                out = out + g[..., None] * (hh @ W2[ei] + b2[ei])
            return out
        key = jax.random.key(seed)
        ks = jax.random.split(key, 8)
        s = 0.05
        return {'x': jax.random.normal(ks[0], (B, N, D), jnp.float32), 'W_gat': jax.random.normal(ks[1], (D, HEADS * NUM_EXPERTS), jnp.float32) * s, 'att_src': jax.random.normal(ks[2], (HEADS, NUM_EXPERTS), jnp.float32) * s, 'att_dst': jax.random.normal(ks[3], (HEADS, NUM_EXPERTS), jnp.float32) * s, 'b_gat': jnp.zeros((HEADS * NUM_EXPERTS,), jnp.float32), 'ln_gamma': jnp.ones((HEADS * NUM_EXPERTS,), jnp.float32), 'ln_beta': jnp.zeros((HEADS * NUM_EXPERTS,), jnp.float32), 'W1': jax.random.normal(ks[4], (NUM_EXPERTS, D, 2 * D), jnp.float32) * s, 'b1': jnp.zeros((NUM_EXPERTS, 2 * D), jnp.float32), 'W2': jax.random.normal(ks[5], (NUM_EXPERTS, 2 * D, D), jnp.float32) * s, 'b2': jnp.zeros((NUM_EXPERTS, D), jnp.float32), 'edge_index': jax.random.randint(ks[6], (2, N_EDGES), 0, B * N, jnp.int32)}
    _L0_ffn_all = _L0_ffn_setup()
    _L0_ffn_in = {k: v for k, v in _L0_ffn_all.items() if k in ('W_gat', 'att_src', 'att_dst', 'b_gat', 'ln_gamma', 'ln_beta', 'W1', 'b1', 'W2', 'b2', 'edge_index')}
    del _L0_ffn_all
    return {'x': x, 'src': src, 'dst': dst, 'L0_gnn_W': _L0_gnn_in['W'], 'L0_gnn_att_src': _L0_gnn_in['att_src'], 'L0_gnn_att_dst': _L0_gnn_in['att_dst'], 'L0_gnn_bias': _L0_gnn_in['bias'], 'L0_gnn_ln_gamma': _L0_gnn_in['ln_gamma'], 'L0_gnn_ln_beta': _L0_gnn_in['ln_beta'], 'L0_ffn_W_gat': _L0_ffn_in['W_gat'], 'L0_ffn_att_src': _L0_ffn_in['att_src'], 'L0_ffn_att_dst': _L0_ffn_in['att_dst'], 'L0_ffn_b_gat': _L0_ffn_in['b_gat'], 'L0_ffn_ln_gamma': _L0_ffn_in['ln_gamma'], 'L0_ffn_ln_beta': _L0_ffn_in['ln_beta'], 'L0_ffn_W1': _L0_ffn_in['W1'], 'L0_ffn_b1': _L0_ffn_in['b1'], 'L0_ffn_W2': _L0_ffn_in['W2'], 'L0_ffn_b2': _L0_ffn_in['b2'], 'L0_ffn_edge_index': _L0_ffn_in['edge_index']}

def reference(x, src, dst, L0_gnn_W, L0_gnn_att_src, L0_gnn_att_dst, L0_gnn_bias, L0_gnn_ln_gamma, L0_gnn_ln_beta, L0_ffn_W_gat, L0_ffn_att_src, L0_ffn_att_dst, L0_ffn_b_gat, L0_ffn_ln_gamma, L0_ffn_ln_beta, L0_ffn_W1, L0_ffn_b1, L0_ffn_W2, L0_ffn_b2, L0_ffn_edge_index):
    import jax
    import jax.numpy as jnp

    def _L0_gnn_ref(x, edge_index, W, att_src, att_dst, bias, ln_gamma, ln_beta):
        import jax, jax.numpy as jnp
        import numpy as np
        N, E = (6250, 100000)
        IN_DIM, HEADS, OUT_DIM = (256, 8, 32)
        NEG_SLOPE = 0.2
        LN_EPS = 1e-05
        n = x.shape[0]
        loop = jnp.arange(n, dtype=edge_index.dtype)
        src = jnp.concatenate([edge_index[0], loop])
        dst = jnp.concatenate([edge_index[1], loop])
        h = (x @ W).reshape(n, HEADS, OUT_DIM)
        a_src = jnp.einsum('nhc,hc->nh', h, att_src)
        a_dst = jnp.einsum('nhc,hc->nh', h, att_dst)
        e = jax.nn.leaky_relu(a_src[src] + a_dst[dst], NEG_SLOPE)
        m = jax.ops.segment_max(e, dst, num_segments=n)
        e = jnp.exp(e - m[dst])
        denom = jax.ops.segment_sum(e, dst, num_segments=n)
        alpha = e / (denom[dst] + 1e-16)
        out = jax.ops.segment_sum(h[src] * alpha[:, :, None], dst, num_segments=n)
        out = out.reshape(n, HEADS * OUT_DIM) + bias
        mu = jnp.mean(out, axis=-1, keepdims=True)
        var = jnp.mean(jnp.square(out - mu), axis=-1, keepdims=True)
        return ln_gamma * (out - mu) * jax.lax.rsqrt(var + LN_EPS) + ln_beta

    def _L0_ffn_ref(x, W_gat, att_src, att_dst, b_gat, ln_gamma, ln_beta, W1, b1, W2, b2, edge_index):
        import jax, jax.numpy as jnp
        import numpy as np
        B, N, D = (16, 512, 256)
        NUM_EXPERTS, TOP_K, HEADS = (4, 2, 4)
        N_EDGES = 131072
        LN_EPS = 1e-05

        def _layernorm(x, g, b):
            mu = x.mean(-1, keepdims=True)
            var = ((x - mu) ** 2).mean(-1, keepdims=True)
            return (x - mu) * jax.lax.rsqrt(var + LN_EPS) * g + b

        def _forward(x, edge_index, W_gat, att_src, att_dst, b_gat, ln_gamma, ln_beta, W1, b1, W2, b2):
            Bc, Nc, Dc = x.shape
            M = Bc * Nc
            x_flat = x.reshape(M, Dc)
            h = (x_flat @ W_gat).reshape(M, HEADS, NUM_EXPERTS)
            loops = jnp.arange(M, dtype=edge_index.dtype)
            src = jnp.concatenate([edge_index[0], loops])
            dst = jnp.concatenate([edge_index[1], loops])
            a_src = (h * att_src).sum(-1)
            a_dst = (h * att_dst).sum(-1)
            e = jax.nn.leaky_relu(a_src[src] + a_dst[dst], negative_slope=0.2)
            e_max = jax.ops.segment_max(e, dst, num_segments=M)
            ee = jnp.exp(e - e_max[dst])
            denom = jax.ops.segment_sum(ee, dst, num_segments=M)
            alpha = ee / (denom[dst] + 1e-16)
            msg = h[src] * alpha[:, :, None]
            agg = jax.ops.segment_sum(msg, dst, num_segments=M).reshape(M, HEADS * NUM_EXPERTS) + b_gat
            scores = _layernorm(agg, ln_gamma, ln_beta).reshape(M, HEADS, NUM_EXPERTS).mean(1)
            scores = scores.reshape(Bc, Nc, NUM_EXPERTS)
            topk_s, topk_i = jax.lax.top_k(scores, TOP_K)
            w = jax.nn.softmax(topk_s, axis=-1)
            out = jnp.zeros_like(x)
            for ei in range(NUM_EXPERTS):
                g = jnp.where(topk_i == ei, w, 0.0).sum(-1)
                hh = jax.nn.gelu(x @ W1[ei] + b1[ei], approximate=False)
                out = out + g[..., None] * (hh @ W2[ei] + b2[ei])
            return out
        return _forward(x, edge_index, W_gat, att_src, att_dst, b_gat, ln_gamma, ln_beta, W1, b1, W2, b2)
    edge_index = jnp.stack([src, dst])
    x = x + _L0_gnn_ref(_layernorm(x, axis=-1), edge_index, L0_gnn_W, L0_gnn_att_src, L0_gnn_att_dst, L0_gnn_bias, L0_gnn_ln_gamma, L0_gnn_ln_beta)
    x = x + _L0_ffn_ref(_layernorm(x, axis=-1)[None], L0_ffn_W_gat, L0_ffn_att_src, L0_ffn_att_dst, L0_ffn_b_gat, L0_ffn_ln_gamma, L0_ffn_ln_beta, L0_ffn_W1, L0_ffn_b1, L0_ffn_W2, L0_ffn_b2, L0_ffn_edge_index)[0]
    return x

_drawn_inputs = setup_inputs


def setup_inputs(seed=0):
    import zlib

    import numpy as np

    out = dict(_drawn_inputs(seed))
    spreads = {'L0_gnn_bias': (0.0, 0.1),
     'L0_gnn_ln_gamma': (1.0, 0.2),
     'L0_gnn_ln_beta': (0.0, 0.1),
     'L0_ffn_b_gat': (0.0, 0.1),
     'L0_ffn_ln_gamma': (1.0, 0.2),
     'L0_ffn_ln_beta': (0.0, 0.1),
     'L0_ffn_b1': (0.0, 0.1),
     'L0_ffn_b2': (0.0, 0.1)}
    factors = {}
    for name, (base, spread) in spreads.items():
        noise = np.random.default_rng([zlib.crc32(name.encode()), seed]).standard_normal(out[name].shape)
        drawn = base * np.exp(spread * noise) if base else spread * noise
        out[name] = jnp.asarray(drawn.astype(out[name].dtype))
    for name, factor in factors.items():
        out[name] = (out[name] * factor).astype(out[name].dtype)
    return out
```

```python
from contextlib import ExitStack

import numpy as np

import concourse.bass as bass
from concourse import mybir
from concourse.alu_op_type import AluOpType as ALU

ACT = mybir.ActivationFunctionType
AX = mybir.AxisListType
F32 = mybir.dt.float32
BF16 = mybir.dt.bfloat16
I32 = mybir.dt.int32
U32 = mybir.dt.uint32

P = 128
N = 6250
D = 256
NB = -(-N // P)
TAIL = N - (NB - 1) * P
EPS = 1e-5
SLOPE = 0.2
SENT = NB * P
LOW = -1e30
OUTSIDE = 1 << 27

HALF = 16
GR = 2 * HALF
GR_LOG = 5
BATCH = 4
NE, FF = 4, 512
FT = FF // P
KT = D // P
FHEADS = 4
TOKB = 4


class Graph:

    def __init__(self, name, edges, heads, width):
        self.name, self.edges, self.heads, self.width = name, edges, heads, width
        self.hc = heads * width
        self.row = self.hc + heads
        tiles = -(-edges // P)
        self.tiles = -(-tiles // (4 * BATCH)) * 4 * BATCH
        self.batches = self.tiles // BATCH
        self.groups = edges // GR + 2 * NB


GNN = Graph("gnn", 100000, 8, 32)
FFN = Graph("ffn", 131072, FHEADS, NE)


def build(nc, x, src, dst, W, att_src, att_dst, bias, gamma, beta, W_gat, fatt_src, fatt_dst, b_gat,
          fgamma, fbeta, W1, b1, W2, b2, edge_index, out):
    ctx = ExitStack()
    with ctx:
        def sb(name, shape, dt=F32):
            return ctx.enter_context(nc.sbuf_tensor(name, shape, dt))

        def sem(name):
            return ctx.enter_context(nc.semaphore(name))

        bank = [ctx.enter_context(nc.psum_tensor(f"bank{i}", [P, 512], F32)) for i in range(8)]

        table = {g.name: nc.dram_tensor(f"table_{g.name}", [SENT + 1, g.row], F32).ap() for g in (GNN, FFN)}
        ell = {g.name: nc.dram_tensor(f"ell_{g.name}", [g.groups * P * GR, 1], U32).ap() for g in (GNN, FFN)}

        acc = sb("acc", [P, NB, GNN.row])
        work = sb("work", [P, NB * D])
        xn_all = work[:, :].rearrange("p (b d) -> p b d", b=NB)
        ring_w = HALF * GNN.row
        ring = {GNN.name: [work[:, s * ring_w:(s + 1) * ring_w].rearrange("p (r w) -> p r w", r=HALF)
                           for s in range(2)]}
        prod_gnn = work[:, 2 * ring_w:2 * ring_w + HALF * GNN.hc].rearrange("p (r w) -> p r w", r=HALF)
        xn2T = work[:, :].rearrange("p (k t) -> p k t", k=KT)
        fring = sb("fring", [P, 2, HALF, FFN.row])
        ring[FFN.name] = [fring[:, s] for s in range(2)]
        fprod = sb("fprod", [P, HALF, FFN.hc])
        prod = {GNN.name: prod_gnn, FFN.name: fprod[:, :, :]}

        facc = sb("facc", [P, NB, FFN.row])
        accs = {GNN.name: acc, FFN.name: facc}
        adst = {g.name: sb(f"adst_{g.name}", [P, NB, g.heads]) for g in (GNN, FFN)}
        mrun = {g.name: sb(f"mrun_{g.name}", [P, NB, g.heads]) for g in (GNN, FFN)}
        tmpm = sb("tmpm", [P, NB, 8])

        TM = FFN.tiles
        edge_buf = sb("edge_buf", [P, 5 * TM], I32)
        dst_i, src_i, t_i, lane_slot = (edge_buf[:, i * TM:(i + 1) * TM] for i in range(4))
        t_f = edge_buf[:, 4 * TM:5 * TM].bitcast(F32)
        hh = edge_buf[:, 0:2 * FT * TOKB * P].bitcast(F32).rearrange("p (s f t) -> p s f t", s=2, f=FT)
        hi_b = sb("hi_b", [P, TM], BF16)
        lo_b = sb("lo_b", [P, TM], BF16)
        OL = sb("OL", [P, 2, BATCH, P], BF16)
        OH = sb("OH", [P, 2, BATCH, NB], BF16)
        Tm = sb("Tm", [P, 2, BATCH, P], BF16)
        OHT = sb("OHT", [NB, 2, BATCH, P])
        Hc = sb("Hc", [NB, 2, P])
        junk = sb("junk", [P, BATCH, P])
        rank = sb("rank", [P, BATCH])
        rank_i = sb("rank_i", [P, BATCH], I32)
        q_i = sb("q_i", [P, BATCH], I32)
        b_i = sb("b_i", [P, BATCH], I32)
        addr = sb("addr", [P, 2, BATCH], U32)
        load = sb("load", [P, 2, BATCH], U32)
        sent_i = sb("sent_i", [P, GR], U32)
        ng = sb("ng", [NB, 1])
        ngi = sb("ngi", [NB, 1], I32)
        ngr = sb("ngr", [NB, P])
        cum = {g.name: sb(f"cum_{g.name}", [1, NB + 1], I32) for g in (GNN, FFN)}
        idx = sb("idx", [P, 2, HALF], U32)

        identf = sb("identf", [P, P])
        identb = sb("identb", [P, P], BF16)
        maskb = sb("maskb", [P, P], BF16)
        upper = sb("upper", [NB, NB + 1])
        iota_f = junk[:, 1, :].bitcast(I32)
        iota_b = sb("iota_b", [P, P], BF16)
        zero_b = sb("zero_b", [P, P], BF16)
        eps_t = sb("eps_t", [P, 1])
        sent_row = sb("sent_row", [1, GNN.row + FFN.row])

        xrow2 = sb("xrow", [P, 2, D])
        wx = sb("wx", [P, KT, D + 16])
        fwx = sb("fwx", [P, KT, 16 + 8])
        attb = xrow2[:, :, :]
        fattb = sb("fattb", [P, 2, 16])
        par = sb("par", [P, 3, D])
        fpar = sb("fpar", [P, 3, 16])
        w1 = sb("w1", [P, KT, NE, FF])
        w2 = sb("w2", [P, FT, NE, D])
        b1t = sb("b1t", [P, NE, FT])
        b2b = sb("b2b", [P, NE, D])

        stats = sb("stats", [P, NB, 6])
        mv = sb("mv", [P, NB, 2])
        rstd = sb("rstd", [P, NB])
        mv2 = sb("mv2", [P, NB, 2])
        xT = sb("xT", [P, 2, KT, P])
        xrow = xrow2
        xnrm = sb("xnrm", [P, 2, D])
        zt = sb("zt", [P, HALF, 8])
        ed = sb("ed", [P, 2, (HALF + 1) * 8])
        wt = sb("wt", [P, 2, (HALF + 1) * 8])
        gm = sb("gm", [P, 8])
        mnew = sb("mnew", [P, 8])
        den_p = sb("den_p", [P, 8])
        part_f = sb("part_f", [P, 16])
        sc = tmpm[:, :, :].rearrange("p b h -> p (b h)")[:, 0:NB * NE].rearrange("p (b e) -> p b e", e=NE)
        cnt = tmpm[:, :, :].rearrange("p b h -> p (b h)")[:, NB * NE:2 * NB * NE].rearrange("p (b e) -> p b e", e=NE)
        cmp = sb("cmp", [P, NB])
        gate = sb("gate", [P, NB, NE])
        lnf = t_f[:, 0:NB * 16].rearrange("p (b c) -> p b c", b=NB)

        s_par = sem("s_par")
        s_att = sem("s_att")
        s_norm = sem("s_norm")
        s_xin = sem("s_xin")
        s_xpad = sem("s_xpad")
        s_const = sem("s_const")
        s_cv = sem("s_cv")
        s_wx = sem("s_wx")
        s_var = sem("s_var")
        s_sd = sem("s_sd")
        st = {}
        for g in (GNN, FFN):
            n = g.name
            st[n] = dict(
                xn=sem(f"{n}_xn_ready"),
                tp=sem(f"{n}_xT_in_psum"),
                tc=sem(f"{n}_xT_copied"),
                pj=sem(f"{n}_proj_done"),
                pc=sem(f"{n}_proj_copied"),
                tab=sem(f"{n}_table_written"),
                acc0=sem(f"{n}_state_ready"),
                raw=sem(f"{n}_edges_landed"),
                fill=sem(f"{n}_edge_pad_written"),
                prep=sem(f"{n}_edges_split"),
                oh=sem(f"{n}_onehots_ready"),
                hist=sem(f"{n}_histogram_batch_done"),
                seeded=sem(f"{n}_histogram_seeded"),
                ng=sem(f"{n}_groups_counted"),
                cumr=sem(f"{n}_group_sums_in_psum"),
                cumw=sem(f"{n}_group_sums_ready"),
                pre=sem(f"{n}_ell_prefilled"),
                oh2=sem(f"{n}_rank_onehots_ready"),
                fr=sem(f"{n}_front_in_psum"),
                oht=sem(f"{n}_onehot_T_copied"),
                tm=sem(f"{n}_pairs_ready"),
                hu=sem(f"{n}_running_histogram_updated"),
                hcp=sem(f"{n}_running_histogram_copied"),
                gr=sem(f"{n}_lookup_ready"),
                ranked=sem(f"{n}_ranks_read"),
                ad=sem(f"{n}_slots_ready"),
                sc=[sem(f"{n}_scattered{s}") for s in range(2)],
                ix=[sem(f"{n}_index_landed{s}") for s in range(2)],
                ga=[sem(f"{n}_rows_landed{s}") for s in range(2)],
                ru=[sem(f"{n}_rows_used{s}") for s in range(2)],
                ed=sem(f"{n}_logits_ready"),
                w=sem(f"{n}_weights_ready"),
                pr=sem(f"{n}_products_ready"),
                ps=sem(f"{n}_products_summed"),
                pa=sem(f"{n}_sums_added"),
                end=sem(f"{n}_attended"),
            )
        s_x2 = [sem(f"s_xrow_landed{s}") for s in range(2)]
        s_x2u = sem("s_xrow_used")
        s_sdo = sem("s_out_var_ready")
        s_sdo2 = sem("s_out_sd_ready")
        s_zf = sem("s_gate_exp_in")
        s_zf2 = sem("s_gate_exp_out")
        s_gate = sem("s_gate_ready")
        s_h1 = sem("s_hidden_in_psum")
        s_h1u = sem("s_hidden_activated")
        s_y = sem("s_expert_out_in_psum")
        s_yu = sem("s_expert_out_added")
        s_hfree = sem("s_hidden_used")
        s_fin = sem("s_block_final")
        s_out = sem("s_out_stored")
        s_step = sem("s_pool_step")

        block = ctx.enter_context(nc.Block())

        def bc(ap, shape):
            return ap.to_broadcast(shape)

        def v_of(psum_bf):
            return psum_bf

        @block.sync
        def _(sp):
            sp.wait_ge(s_xpad, 1)
            sp.dma_start(xn_all[:, 0:NB - 1, :], x[0:(NB - 1) * P, :].rearrange("(b p) d -> p b d", p=P)).then_inc(s_xin, 16)
            sp.dma_start(xn_all[0:TAIL, NB - 1, :], x[(NB - 1) * P:N, :]).then_inc(s_xin, 16)
            sp.dma_start(wx[:, :, 0:D], W.rearrange("(k p) n -> p k n", p=P)).then_inc(s_att, 16)
            sp.dma_start(attb[:, 0, :], att_src.rearrange("(a h) c -> a (h c)", a=1).to_broadcast([P, D])).then_inc(s_att, 16)
            sp.dma_start(attb[:, 1, :], att_dst.rearrange("(a h) c -> a (h c)", a=1).to_broadcast([P, D])).then_inc(s_att, 16)
            sp.dma_start(fwx[:, :, 0:16], W_gat.rearrange("(k p) n -> p k n", p=P)).then_inc(s_att, 16)
            sp.dma_start(fattb[:, 0, :], fatt_src.rearrange("(a h) c -> a (h c)", a=1).to_broadcast([P, 16])).then_inc(s_att, 16)
            sp.dma_start(fattb[:, 1, :], fatt_dst.rearrange("(a h) c -> a (h c)", a=1).to_broadcast([P, 16])).then_inc(s_att, 16)
            raw = st["gnn"]["raw"]
            T = GNN.tiles
            full = GNN.edges // T
            rest = GNN.edges - full * T
            sp.wait_ge(st["gnn"]["fill"], 1)
            for to, of in ((dst_i, dst), (src_i, src)):
                sp.dma_start(to[0:full, 0:T], of[0:full * T].rearrange("(p t) -> p t", t=T)).then_inc(raw, 16)
                sp.dma_start(to[full:full + 1, 0:rest], of[full * T:GNN.edges].rearrange("(p t) -> p t", p=1)).then_inc(raw, 16)
            for i, v in enumerate((bias, gamma, beta)):
                sp.dma_start(par[:, i, :], v.rearrange("(a d) -> a d", a=1).to_broadcast([P, D])).then_inc(s_norm, 16)
            for i, v in enumerate((b_gat, fgamma, fbeta)):
                sp.dma_start(fpar[:, i, :], v.rearrange("(a d) -> a d", a=1).to_broadcast([P, 16])).then_inc(s_norm, 16)
            for e in range(NE):
                sp.dma_start(w1[:, :, e, :], W1[e].rearrange("(k p) f -> p k f", p=P)).then_inc(s_par, 16)
                sp.dma_start(w2[:, :, e, :], W2[e].rearrange("(f p) d -> p f d", p=P)).then_inc(s_par, 16)
                sp.dma_start(b2b[:, e, :], b2[e:e + 1, :].to_broadcast([P, D])).then_inc(s_par, 16)
            with nc.allow_non_contiguous_dma(reason="b1 by hidden unit on the partitions"):
                sp.dma_start(b1t[:, :, :], b1.rearrange("e (f p) -> p e f", p=P)).then_inc(s_par, 16)

            def tables(g, off):
                s = st[g.name]
                sp.wait_ge(s["pc"], NB)
                sp.dma_start(table[g.name][0:SENT, :].rearrange("(b p) w -> p b w", p=P), accs[g.name][:, :, :]).then_inc(s["tab"], 16)
                sp.dma_start(table[g.name][SENT:SENT + 1, :], sent_row[:, off:off + g.row]).then_inc(s["tab"], 16)

            def prefill(g):
                s = st[g.name]
                sp.wait_ge(s["cumw"], 1)
                total = sp.value_load(cum[g.name][0:1, NB:NB + 1], min_val=NB, max_val=g.groups)
                with sp.Fori(0, total) as i:
                    sp.dma_start(ell[g.name][bass.ds(i * (P * GR), P * GR), :].rearrange("(p r) o -> p (r o)", p=P),
                                 sent_i[:, :]).then_inc(s["pre"], 16)
                sp.wait_ge(s["pre"], total * 16)
                sp.sem_inc(s["cumw"], 1)

            def indices(g):
                s = st[g.name]
                for h in range(2):
                    sp.wait_ge(s["sc"][h], 16 * BATCH * (g.batches // 2))
                total = sp.value_load(cum[g.name][0:1, NB:NB + 1], min_val=NB, max_val=g.groups)
                with sp.Fori(0, total) as i:
                    for h in range(2):
                        sp.wait_ge(s["ga"][h], i * (16 * HALF))
                        sp.dma_start(idx[:, h, :], ell[g.name][bass.ds(i * (P * GR), P * GR), :].rearrange("(p r) o -> p (r o)", p=P)[:, h * HALF:(h + 1) * HALF]).then_inc(s["ix"][h], 16)

            sp.wait_ge(s_cv, 1)
            sp.wait_ge(s_const, 1)
            prefill(GNN)
            tables(GNN, 0)
            indices(GNN)
            sp.wait_ge(st["gnn"]["end"], 1)
            for b in range(2):
                sp.dma_start(xrow[:, b, :], x[b * P:(b + 1) * P, :]).then_inc(s_x2[b], 16)
            with sp.Fori(1, (NB - 1) // 2) as i:
                for h in range(2):
                    sp.wait_ge(s_x2u, 2 * i + h - 1)
                    sp.dma_start(xrow[:, h, :], x[bass.ds((2 * i + h) * P, P), :]).then_inc(s_x2[h], 16)
            sp.wait_ge(s_x2u, NB - 2)
            sp.dma_start(xrow[0:TAIL, 0, :], x[(NB - 1) * P:N, :]).then_inc(s_x2[0], 16)
            sp.wait_ge(st["gnn"]["sc"][0], 16 * BATCH * (GNN.batches // 2))
            sp.wait_ge(st["gnn"]["sc"][1], 16 * BATCH * (GNN.batches // 2))
            T = FFN.tiles
            sp.dma_start(dst_i[:, :], edge_index[1].rearrange("(p t) -> p t", t=T)).then_inc(st["ffn"]["raw"], 16)
            sp.dma_start(src_i[:, :], edge_index[0].rearrange("(p t) -> p t", t=T)).then_inc(st["ffn"]["raw"], 16)
            prefill(FFN)
            tables(FFN, GNN.row)
            indices(FFN)
            with sp.Fori(0, NB - 1) as b:
                sp.wait_ge(s_fin, b + 1)
                sp.dma_start(out[bass.ds(b * P, P), :], acc[:, bass.ds(b, 1), 0:D].rearrange("p a d -> p (a d)")).then_inc(s_out, 16)
            sp.wait_ge(s_fin, NB)
            sp.dma_start(out[(NB - 1) * P:N, :], acc[0:TAIL, NB - 1, 0:D]).then_inc(s_out, 16)
            sp.wait_ge(s_out, 16 * NB)

        @block.gpsimd
        def _(pool):
            pool.memset(identf[:, :], 0.0)
            pool.memset(upper[:, :], 1.0)
            pool.memset(sent_row[:, :], 0.0)
            pool.drain()
            pool.memset(sent_row[0:1, GNN.hc:GNN.row], LOW)
            pool.memset(sent_row[0:1, GNN.row + FFN.hc:GNN.row + FFN.row], LOW)
            pool.iota(iota_f[:, :], pattern=[[1, P]], base=0, channel_multiplier=0)
            pool.iota(sent_i[:, :], pattern=[[0, GR]], base=SENT, channel_multiplier=0)
            pool.affine_select(out=identf[:, :], in_=identf[:, :], compare_op=ALU.not_equal, fill=1.0,
                               base=0, pattern=[[-1, P]], channel_multiplier=1)
            pool.affine_select(out=upper[:, :], in_=upper[:, :], compare_op=ALU.is_gt, fill=0.0,
                               base=0, pattern=[[1, NB + 1]], channel_multiplier=-1)
            pool.memset(junk[:, 0, :], float(1 << 20))
            pool.drain()
            pool.affine_select(out=junk[:, 0, :], in_=junk[:, 0, :], compare_op=ALU.is_ge, fill=0.0,
                               base=0, pattern=[[-1, P]], channel_multiplier=1)
            pool.drain().then_inc(s_const, 1)

            def scatters(g):
                s = st[g.name]
                pool.wait_ge(s["cumw"], 2)
                with pool.Fori(0, g.batches // 2) as i:
                    for h in range(2):
                        pool.wait_ge(s["ad"], 2 * i + h + 1)
                        pool.sem_inc(s_step, 1)
                        for k in range(BATCH):
                            pool.indirect_dma_start(ell[g.name], bass.IndirectOffsetOnAxis(addr[:, h, k:k + 1], 0),
                                                    load[:, h, k:k + 1], None, bounds_check=g.groups * P * GR - 1,
                                                    oob_is_err=False).then_inc(s["sc"][h], 16)

            def gathers(g):
                s = st[g.name]
                pool.wait_ge(s["acc0"], 1)
                pool.wait_ge(s["tab"], 32)
                pool.wait_ge(s["cumw"], 1)
                total = pool.value_load(cum[g.name][0:1, NB:NB + 1], min_val=NB, max_val=g.groups)
                with pool.Fori(0, total) as i:
                    for h in range(2):
                        pool.wait_ge(s["ix"][h], (i + 1) * 16)
                        pool.wait_ge(s["ru"][h], i)
                        pool.sem_inc(s_step, 1)
                        for r in range(HALF):
                            pool.indirect_dma_start(ring[g.name][h][:, r, :], None, table[g.name],
                                                    bass.IndirectOffsetOnAxis(idx[:, h, r:r + 1], 0)).then_inc(s["ga"][h], 16)

            scatters(GNN)
            gathers(GNN)
            scatters(FFN)
            gathers(FFN)

        @block.scalar
        def _(act):
            def proj(g, stage):
                s = st[g.name]
                act.wait_ge(s_var, stage)
                act.activation(rstd[:, :], (mv if stage == 1 else mv2)[:, :, 1], ACT.Sqrt, bias=eps_t[:, 0:1]).then_inc(s_sd, 1)
                def copy(b, h):
                    act.wait_ge(s["tp"], b + 1)
                    if not isinstance(b, int) or b >= 2:
                        act.wait_ge(s["pj"], b - 1)
                    rows_t = bank[h][:, 0:D].rearrange("p (k t) -> p k t", k=KT)
                    if stage == 2:
                        act.activation(xn2T[:, :, bass.ds(b * P, P)], rows_t, ACT.Copy)
                    act.activation(xT[:, h], rows_t, ACT.Copy).then_inc(s["tc"], 1)
                copy(0, 0)
                copy(1, 1)
                with act.Fori(1, (NB - 1) // 2) as i:
                    for h in range(2):
                        copy(2 * i + h, h)
                copy(NB - 1, 0)

            def ranks(g):
                s = st[g.name]
                act.wait_ge(s["seeded"], 2)
                act.activation(Hc[:, 0, :], bank[0][0:NB, 0:P], ACT.Copy).then_inc(s["hcp"], 1)

                def onehot(n, h):
                    act.wait_ge(s["fr"], n + 1)
                    act.activation(OHT[:, h], bank[5 + h][0:NB, 0:BATCH * P // 2].bitcast(BF16).rearrange("p (k e) -> p k e", k=BATCH), ACT.Copy).then_inc(s["oht"], 1)

                def chain(n):
                    for k in range(BATCH):
                        act.wait_ge(s["hu"], n * BATCH + k + 1)
                        act.activation(Hc[:, (k + 1) % 2, :], bank[0][0:NB, 0:P], ACT.Copy).then_inc(s["hcp"], 1)

                onehot(0, 0)
                with act.Fori(0, g.batches // 2 - 1) as i:
                    for h in range(2):
                        onehot(2 * i + h + 1, 1 - h)
                        chain(2 * i + h)
                onehot(g.batches - 1, 1)
                chain(g.batches - 2)
                chain(g.batches - 1)

            def weights(g):
                s = st[g.name]
                w = (HALF + 1) * g.heads
                act.wait_ge(s["cumw"], 1)
                total = act.value_load(cum[g.name][0:1, NB:NB + 1], min_val=NB, max_val=g.groups)
                with act.Fori(0, total) as i:
                    for h in range(2):
                        act.wait_ge(s["ed"], 2 * i + h + 1)
                        act.activation(wt[:, h, 0:w], ed[:, h, 0:w], ACT.Exp).then_inc(s["w"], 1)

            act.wait_ge(s_cv, 1)
            proj(GNN, 1)
            ranks(GNN)
            weights(GNN)
            def out_sd(b, h):
                act.wait_ge(s_sdo, b + 1)
                act.activation(rstd[:, h:h + 1], mv[:, h, 1:2], ACT.Sqrt, bias=eps_t[:, 0:1]).then_inc(s_sdo2, 1)

            with act.Fori(0, (NB - 1) // 2) as i:
                for h in range(2):
                    out_sd(2 * i + h, h)
            out_sd(NB - 1, 0)
            proj(FFN, 2)
            ranks(FFN)
            weights(FFN)
            act.wait_ge(s_zf, 1)
            act.activation(rstd[:, :], mv2[:, :, 1], ACT.Sqrt, bias=eps_t[:, 0:1]).then_inc(s_zf2, 1)
            act.wait_ge(s_zf, 2)
            act.activation(gate[:, :, :], sc[:, :, :], ACT.Exp).then_inc(s_zf2, 1)

            def expert(n, e, cols):
                for f in range(FT):
                    act.wait_ge(s_h1, (n * FT) + f + 1)
                    if f == 0 and (not isinstance(n, int) or n >= 2):
                        act.wait_ge(s_hfree, n - 1)
                    act.activation(hh[:, e % 2, f, 0:cols], bank[f][:, 0:cols], ACT.Gelu, bias=b1t[:, e, f:f + 1]).then_inc(s_h1u, 1)

            for e in range(NE):
                expert(e, e, TOKB * P)
            with act.Fori(1, NB // TOKB) as i:
                for e in range(NE):
                    expert(i * NE + e, e, TOKB * P)
            for e in range(NE):
                expert((NB // TOKB) * NE + e, e, P)

        @block.tensor
        def _(pe):
            def proj(g, stage):
                s = st[g.name]
                ncol = g.row + g.heads
                wgt = wx if stage == 1 else fwx

                def block_of(b, h):
                    pe.wait_ge(s["xn"], b + 1)
                    if not isinstance(b, int) or b >= 2:
                        pe.wait_ge(s["tc"], b - 1)
                        pe.wait_ge(s["pc"], b - 1)
                    for k in range(KT):
                        t = pe.transpose(bank[h][:, k * P:(k + 1) * P], xnrm[:, h, k * P:(k + 1) * P], identf[:, :])
                    t.then_inc(s["tp"], 1)
                    pe.wait_ge(s["tc"], b + 1)
                    for k in range(KT):
                        m = pe.matmul(bank[2 + h][:, 0:ncol], xT[:, h, k, :], wgt[:, k, 0:ncol], start=(k == 0), stop=(k == KT - 1))
                    m.then_inc(s["pj"], 1)

                block_of(0, 0)
                block_of(1, 1)
                with pe.Fori(1, (NB - 1) // 2) as i:
                    for h in range(2):
                        block_of(2 * i + h, h)
                block_of(NB - 1, 0)

            def histogram(g):
                s = st[g.name]
                pe.matmul(bank[0][0:NB, 0:P], zero_b[:, 0:NB], zero_b[:, :], start=True, stop=False, skip_group_check=True)
                with pe.Fori(0, g.batches // 2) as i:
                    for h in range(2):
                        pe.wait_ge(s["oh"], 2 * i + h + 1)
                        for k in range(BATCH):
                            m = pe.matmul(bank[0][0:NB, 0:P], OH[:, h, k, :], OL[:, h, k, :], start=False, stop=False, skip_group_check=True)
                        m.then_inc(s["hist"], 1)
                pe.wait_ge(s["ng"], 1)
                pe.matmul(bank[1][0:1, 0:NB + 1], ng[:, 0:1], upper[:, :], start=True, stop=True).then_inc(s["cumr"], 1)
                pe.matmul(bank[0][0:NB, 0:P], upper[:, 0:NB], ngr[:, :], start=True, stop=True, skip_group_check=True).then_inc(s["seeded"], 2)

            def ranks(g):
                s = st[g.name]

                def front(n, h):
                    pe.wait_ge(s["oh2"], n + 1)
                    if not isinstance(n, int) or n >= 2:
                        pe.wait_ge(s["tm"], n - 1)
                        pe.wait_ge(s["oht"], n - 1)
                    for k in range(BATCH):
                        pe.matmul(bank[3 + h][:, k * P:(k + 1) * P], bc(hi_b[:, bass.ds(n * BATCH + k, 1)], [P, P]), identb[:, :],
                                  start=True, stop=False, skip_group_check=True)
                        pe.matmul(bank[3 + h][:, k * P:(k + 1) * P], identb[:, :], maskb[:, :], start=False, stop=True, skip_group_check=True)
                    for k in range(BATCH):
                        t = pe.transpose(bank[5 + h][0:NB, k * P // 2:(k + 1) * P // 2].bitcast(BF16), OH[:, h, k, :], identb[:, :])
                    t.then_inc(s["fr"], 1)

                def chain(n, h):
                    pe.wait_ge(s["oht"], n + 1)
                    pe.wait_ge(s["tm"], n + 1)
                    pe.wait_ge(s["ranked"], n + 1)
                    for k in range(BATCH):
                        pe.wait_ge(s["hcp"], n * BATCH + k + 1)
                        pe.matmul(bank[1 + h][:, k * P:(k + 1) * P], OHT[:, h, k, :], Hc[:, k % 2, :], start=True, stop=False, skip_group_check=True)
                        m = pe.matmul(bank[1 + h][:, k * P:(k + 1) * P], Tm[:, h, k, :], OL[:, h, k, :], start=False, stop=True, skip_group_check=True)
                        if k == BATCH - 1:
                            m.then_inc(s["gr"], 1)
                        pe.matmul(bank[0][0:NB, 0:P], OH[:, h, k, :], OL[:, h, k, :], start=False, stop=False, skip_group_check=True).then_inc(s["hu"], 1)

                front(0, 0)
                with pe.Fori(0, g.batches // 2 - 1) as i:
                    for h in range(2):
                        front(2 * i + h + 1, 1 - h)
                        chain(2 * i + h, h)
                front(g.batches - 1, 1)
                chain(g.batches - 2, 0)
                chain(g.batches - 1, 1)

            def sums(g):
                s = st[g.name]
                pe.wait_ge(s["cumw"], 1)
                total = pe.value_load(cum[g.name][0:1, NB:NB + 1], min_val=NB, max_val=g.groups)
                with pe.Fori(0, total) as i:
                    for h in range(2):
                        pe.wait_ge(s["pr"], 2 * i + h + 1)
                        pe.wait_ge(s["pa"], 2 * i + h)
                        for r in range(HALF):
                            m = pe.matmul(bank[7][:, 0:g.hc], identf[:, :], prod[g.name][:, r, :], start=(r == 0), stop=(r == HALF - 1))
                        m.then_inc(s["ps"], 1)

            pe.wait_ge(s_const, 1)
            pe.wait_ge(s_cv, 2)
            pe.wait_ge(s_wx, 1)
            proj(GNN, 1)
            pe.wait_ge(st["gnn"]["pc"], NB)
            histogram(GNN)
            ranks(GNN)
            sums(GNN)
            pe.wait_ge(st["gnn"]["ranked"], GNN.batches + 2)
            proj(FFN, 2)
            pe.wait_ge(st["ffn"]["pc"], NB)
            histogram(FFN)
            ranks(FFN)

            pe.wait_ge(s_par, 16 * (3 * NE + 1))
            pe.wait_ge(st["ffn"]["ranked"], FFN.batches + 2)
            pe.wait_ge(st["ffn"]["hcp"], FFN.tiles + 1)
            pe.wait_ge(s_gate, 1)

            def expert(n, e, b0, nblk):
                cols = nblk * P
                for f in range(FT):
                    if not isinstance(n, int) or n >= 1:
                        if not (e == 0 and isinstance(n, int)):
                            pass
                    pe.wait_ge(s_h1u, n * FT - (FT - 1 - f)) if n_first[0] is False else None
                    for k in range(KT):
                        m = pe.matmul(bank[f][:, 0:cols], w1[:, k, e, f * P:(f + 1) * P], xn2T[:, k, bass.ds(b0 * P, cols)],
                                      start=(k == 0), stop=(k == KT - 1))
                    m.then_inc(s_h1, 1)
                pe.wait_ge(s_h1u, (n + 1) * FT)
                for j in range(nblk):
                    o = bank[4 + j][:, 0:D]
                    y = n * TOKB + j if nblk == TOKB else None
                    if nblk == TOKB:
                        pe.wait_ge(s_yu, n * TOKB + j - (TOKB - 1)) if n_first[0] is False else None
                    else:
                        pe.wait_ge(s_yu, (NB // TOKB) * NE * TOKB + e)
                    for f in range(FT):
                        m = pe.matmul(o, hh[:, e % 2, f, j * P:(j + 1) * P], w2[:, f, e, :], start=(f == 0), stop=(f == FT - 1))
                    m.then_inc(s_y, 1)
                    if j == nblk - 1:
                        pass
                m2 = pe.drain().then_inc(s_hfree, 1)

            n_first = [True]
            for e in range(NE):
                expert(e, e, 0, TOKB)
                n_first[0] = False
            with pe.Fori(1, NB // TOKB) as i:
                for e in range(NE):
                    expert(i * NE + e, e, i * TOKB, TOKB)
            for e in range(NE):
                expert((NB // TOKB) * NE + e, e, (NB // TOKB) * TOKB, NB - (NB // TOKB) * TOKB)

        @block.vector
        def _(v):
            v.memset(xn_all[:, NB - 1, :], 0.0)
            v.drain().then_inc(s_xpad, 1)
            v.memset(dst_i[:, :], -1)
            v.memset(src_i[:, :], 0)
            v.drain().then_inc(st["gnn"]["fill"], 1)
            v.memset(eps_t[:, :], EPS)
            v.memset(zero_b[:, :], 0.0)
            v.drain().then_inc(s_cv, 1)
            v.wait_ge(s_const, 1)
            v.tensor_copy(iota_b[:, :], iota_f[:, :])
            v.tensor_copy(identb[:, :], identf[:, :])
            v.tensor_copy(maskb[:, :], junk[:, 0, :])
            v.drain().then_inc(s_cv, 1)
            v.wait_ge(s_att, 16 * 6)
            tmpw = t_f[:, 0:D]
            for (wgt, at, g) in ((wx, attb, GNN), (fwx, fattb, FFN)):
                for k in range(KT):
                    for a in range(2):
                        v.tensor_tensor(tmpw[:, 0:g.hc], wgt[:, k, 0:g.hc], at[:, a, :], ALU.mult)
                        v.drain()
                        v.tensor_reduce(wgt[:, k, g.hc + a * g.heads:g.hc + (a + 1) * g.heads],
                                        tmpw[:, 0:g.hc].rearrange("p (h c) -> p h c", c=g.width), AX.X, ALU.add)
                        v.drain()
            v.drain().then_inc(s_wx, 1)

            def mean_var(of, b):
                v.bn_stats(stats[:, bass.ds(b, 1), :].rearrange("p a s -> p (a s)"), of)

            def blk(t, b, lo=0, hi=None):
                return t[:, bass.ds(b, 1), lo:hi if hi is not None else t.shape[2]].rearrange("p a d -> p (a d)")

            def state(g):
                s = st[g.name]
                a = accs[g.name]
                v.wait_ge(s["tab"], 32)
                tm = tmpm[:, :, 0:g.heads]
                v.tensor_tensor(tm, a[:, :, g.hc:g.row], adst[g.name][:, :, :], ALU.add)
                v.drain()
                v.scalar_tensor_tensor(out=mrun[g.name][:, :, :], in0=tm, scalar=SLOPE, in1=tm, op0=ALU.mult, op1=ALU.max)
                v.memset(a[:, :, g.hc:g.row], 1.0)
                v.drain().then_inc(s["acc0"], 1)

            def proj_out(g, b, h):
                s = st[g.name]
                v.wait_ge(s["pj"], b + 1)
                v.tensor_copy(blk(accs[g.name], b), bank[2 + h][:, 0:g.row])
                v.tensor_copy(blk(adst[g.name], b), bank[2 + h][:, g.row:g.row + g.heads])
                v.drain().then_inc(s["pc"], 1)

            def normalise(g, of, mean):
                s = st[g.name]

                def norm(b, h):
                    if not isinstance(b, int) or b >= 2:
                        v.wait_ge(s["tp"], b - 1)
                    v.tensor_scalar(xnrm[:, h, :], blk(of, b, 0, D), blk(mean, b, 0, 1), rstd[:, bass.ds(b, 1)], ALU.subtract, ALU.mult)
                    v.drain().then_inc(s["xn"], 1)

                norm(0, 0)
                norm(1, 1)
                proj_out(g, 0, 0)
                with v.Fori(1, (NB - 1) // 2) as i:
                    for h in range(2):
                        norm(2 * i + h, h)
                        proj_out(g, 2 * i + h - 1, 1 - h)
                norm(NB - 1, 0)
                proj_out(g, NB - 2, 1)
                proj_out(g, NB - 1, 0)

            def sort(g):
                s = st[g.name]
                T = g.tiles
                v.wait_ge(s["raw"], 64 if g is GNN else 32)
                di, si, ti, tf = dst_i[:, 0:T], src_i[:, 0:T], t_i[:, 0:T], t_f[:, 0:T]
                v.tensor_scalar(ti, di, 7, None, ALU.logical_shift_right)
                v.tensor_scalar(di, di, P - 1, None, ALU.bitwise_and)
                v.drain()
                v.tensor_copy(hi_b[:, 0:T], ti)
                v.tensor_copy(lo_b[:, 0:T], di)
                v.tensor_scalar(lane_slot[:, 0:T], ti, float(NB), float(OUTSIDE), ALU.is_ge, ALU.mult)
                v.drain()
                v.tensor_scalar(ti, di, GR_LOG, None, ALU.logical_shift_left)
                v.drain()
                v.tensor_tensor(lane_slot[:, 0:T], lane_slot[:, 0:T], ti, ALU.bitwise_or)
                v.tensor_scalar(tf, si, 0.0, float(N), ALU.is_lt, ALU.mult)
                v.drain()
                v.tensor_tensor(tf, si, tf, ALU.add)
                v.drain()
                v.tensor_scalar(si, tf, 0.0, float(N - 1), ALU.max, ALU.min)
                v.drain()

                def onehots(n, h):
                    v.tensor_tensor(OL[:, h], bc(iota_b[:, 0:P].unsqueeze(1), [P, BATCH, P]),
                                    bc(lo_b[:, bass.ds(n * BATCH, BATCH)].unsqueeze(2), [P, BATCH, P]), ALU.is_equal)
                    v.tensor_tensor(OH[:, h], bc(iota_b[:, 0:NB].unsqueeze(1), [P, BATCH, NB]),
                                    bc(hi_b[:, bass.ds(n * BATCH, BATCH)].unsqueeze(2), [P, BATCH, NB]), ALU.is_equal)

                with v.Fori(0, g.batches // 2) as i:
                    for h in range(2):
                        v.wait_ge(s["hist"], (2 * i + h) - 1) if h else v.wait_ge(s["hist"], 2 * i - 0) if False else None
                        if h == 0:
                            v.wait_ge(s["hist"], 2 * i)
                        onehots(2 * i + h, h)
                        v.drain().then_inc(s["oh"], 1)
                v.wait_ge(s["hist"], g.batches)
                v.tensor_reduce(ng[:, :], bank[0][0:NB, 0:P], AX.X, ALU.max)
                v.drain()
                v.tensor_scalar(ngi[:, :], ng[:, :], 1.0, float(GR - 1), ALU.max, ALU.add)
                v.drain()
                v.tensor_scalar(ngi[:, :], ngi[:, :], GR_LOG, None, ALU.logical_shift_right)
                v.drain()
                v.tensor_copy(ng[:, :], ngi[:, :])
                v.drain()
                v.tensor_scalar(ngr[:, :], bc(ng[:, :], [NB, P]), float(GR), None, ALU.mult)
                v.drain().then_inc(s["ng"], 1)
                v.wait_ge(s["cumr"], 1)
                v.tensor_copy(cum[g.name][:, :], bank[1][0:1, 0:NB + 1])
                v.drain().then_inc(s["cumw"], 1)
                v.engine_nop().then_inc(s["ranked"], 2)

                def front(n, h):
                    if not isinstance(n, int) or n >= 1:
                        v.wait_ge(s["gr"], n - 1)
                    if not isinstance(n, int) or n >= 2:
                        v.wait_ge(s["hu"], (n - 1) * BATCH)
                    onehots(n, h)
                    v.drain().then_inc(s["oh2"], 1)

                def pairs(n, h):
                    v.wait_ge(s["fr"], n + 1)
                    v.tensor_tensor(Tm[:, h], bank[3 + h][:, :].rearrange("p (k e) -> p k e", k=BATCH),
                                    bc(hi_b[:, bass.ds(n * BATCH, BATCH)].unsqueeze(2), [P, BATCH, P]), ALU.is_equal)
                    v.drain().then_inc(s["tm"], 1)

                def rank_of(n, h, i):
                    v.wait_ge(s["gr"], n + 1)
                    for k in range(BATCH):
                        v.scalar_tensor_tensor(out=junk[:, k, :], in0=bank[1 + h][:, k * P:(k + 1) * P], scalar=1.0,
                                               in1=OL[:, h, k, :], op0=ALU.mult, op1=ALU.mult, accum_out=rank[:, k:k + 1])
                    v.drain().then_inc(s["ranked"], 1)
                    v.tensor_copy(rank_i[:, :], rank[:, :])
                    v.drain()
                    v.wait_ge(s["sc"][h], i * (16 * BATCH))
                    v.tensor_scalar(q_i[:, :], rank_i[:, :], GR_LOG, GR_LOG + 7, ALU.logical_shift_right, ALU.logical_shift_left)
                    v.scalar_tensor_tensor(out=b_i[:, :], in0=rank_i[:, :], scalar=GR - 1,
                                           in1=lane_slot[:, bass.ds(n * BATCH, BATCH)], op0=ALU.bitwise_and, op1=ALU.bitwise_or)
                    v.tensor_copy(load[:, h, :], src_i[:, bass.ds(n * BATCH, BATCH)])
                    v.drain()
                    v.tensor_tensor(addr[:, h, :], q_i[:, :].bitcast(U32), b_i[:, :].bitcast(U32), ALU.bitwise_or)
                    v.drain().then_inc(s["ad"], 1)

                front(0, 0)
                pairs(0, 0)
                with v.Fori(0, g.batches // 2 - 1) as i:
                    for h in range(2):
                        front(2 * i + h + 1, 1 - h)
                        pairs(2 * i + h + 1, 1 - h)
                        rank_of(2 * i + h, h, i)
                front(g.batches - 1, 1)
                pairs(g.batches - 1, 1)
                rank_of(g.batches - 2, 0, g.batches // 2 - 1)
                rank_of(g.batches - 1, 1, g.batches // 2 - 1)

            def attend(g, on_pe):
                s = st[g.name]
                H, C, HC = g.heads, g.width, g.hc
                a, m = accs[g.name], mrun[g.name]
                pr = prod[g.name]
                z = zt[:, :, 0:H]
                with v.Fori(0, NB) as b:
                    first = v.value_load(cum[g.name][0:1, bass.ds(b, 1)], min_val=0, max_val=g.groups - 1)
                    last = v.value_load(cum[g.name][0:1, bass.ds(b + 1, 1)], min_val=1, max_val=g.groups)
                    with v.Fori(first, last) as i:
                        for h in range(2):
                            rows = ring[g.name][h]
                            e_ = ed[:, h, 0:HALF * H].rearrange("p (r h) -> p r h", r=HALF)
                            w_ = wt[:, h, 0:HALF * H].rearrange("p (r h) -> p r h", r=HALF)
                            old = ed[:, h, HALF * H:(HALF + 1) * H]
                            sc_ = wt[:, h, HALF * H:(HALF + 1) * H]
                            v.wait_ge(s["ga"][h], (i + 1) * (16 * HALF))
                            v.tensor_tensor(z, rows[:, :, HC:HC + H], bc(blk(adst[g.name], b).unsqueeze(1), [P, HALF, H]), ALU.add)
                            v.drain()
                            v.scalar_tensor_tensor(out=e_, in0=z, scalar=SLOPE, in1=z, op0=ALU.mult, op1=ALU.max)
                            v.drain()
                            v.tensor_reduce(gm[:, 0:H], e_.rearrange("p r h -> p h r"), AX.X, ALU.max)
                            v.drain()
                            v.tensor_tensor(mnew[:, 0:H], gm[:, 0:H], blk(m, b), ALU.max)
                            v.drain()
                            v.tensor_tensor(e_, e_, bc(mnew[:, 0:H].unsqueeze(1), [P, HALF, H]), ALU.subtract)
                            v.tensor_tensor(old, blk(m, b), mnew[:, 0:H], ALU.subtract)
                            v.drain().then_inc(s["ed"], 1)
                            v.tensor_copy(blk(m, b), mnew[:, 0:H])
                            v.wait_ge(s["w"], 2 * i + h + 1)
                            if on_pe:
                                v.wait_ge(s["ps"], 2 * i + h)
                            v.tensor_tensor(pr.rearrange("p r (h c) -> p r h c", c=C),
                                            rows[:, :, 0:HC].rearrange("p r (h c) -> p r h c", c=C),
                                            bc(w_.unsqueeze(3), [P, HALF, H, C]), ALU.mult)
                            v.drain().then_inc(s["ru"][h], 1)
                            if on_pe:
                                v.engine_nop().then_inc(s["pr"], 1)
                            v.tensor_reduce(den_p[:, 0:H], w_.rearrange("p r h -> p h r"), AX.X, ALU.add)
                            v.tensor_tensor(blk(a, b, 0, HC).rearrange("p (h c) -> p h c", c=C),
                                            blk(a, b, 0, HC).rearrange("p (h c) -> p h c", c=C),
                                            bc(sc_.unsqueeze(2), [P, H, C]), ALU.mult)
                            v.tensor_tensor(blk(a, b, HC, HC + H), blk(a, b, HC, HC + H), sc_, ALU.mult)
                            if not on_pe:
                                v.tensor_reduce(part_f[:, 0:HC], pr.rearrange("p r w -> p w r"), AX.X, ALU.add)
                            v.drain()
                            v.tensor_tensor(blk(a, b, HC, HC + H), blk(a, b, HC, HC + H), den_p[:, 0:H], ALU.add)
                            if on_pe:
                                v.wait_ge(s["ps"], 2 * i + h + 1)
                                v.tensor_tensor(blk(a, b, 0, HC), blk(a, b, 0, HC), bank[7][:, 0:HC], ALU.add)
                                v.drain().then_inc(s["pa"], 1)
                            else:
                                v.tensor_tensor(blk(a, b, 0, HC), blk(a, b, 0, HC), part_f[:, 0:HC], ALU.add)
                                v.drain()

            v.wait_ge(s_xin, 32)
            with v.Fori(0, NB // 7) as i:
                for j in range(7):
                    mean_var(blk(xn_all, i * 7 + j), i * 7 + j)
            v.drain()
            for b in range(NB):
                v.bn_aggr(mv[:, b, :], stats[:, b, :])
            v.drain().then_inc(s_var, 1)
            v.wait_ge(s_sd, 1)
            v.reciprocal(rstd[:, :], rstd[:, :])
            v.drain()
            normalise(GNN, xn_all, mv)
            sort(GNN)
            v.wait_ge(s_norm, 16 * 6)
            state(GNN)
            attend(GNN, True)

            v.drain().then_inc(st["gnn"]["end"], 1)

            def finish(b, h, use, rows=P):
                o = blk(acc, b, 0, D)
                dn = blk(acc, b, D, GNN.row)
                v.tensor_scalar(dn, dn, 1e-16, None, ALU.add)
                v.drain()
                v.reciprocal(dn, dn)
                v.drain()
                v.tensor_tensor(o.rearrange("p (h c) -> p h c", h=8), o.rearrange("p (h c) -> p h c", h=8),
                                bc(dn.unsqueeze(2), [P, 8, 32]), ALU.mult)
                v.drain()
                v.tensor_tensor(o, o, par[:, 0, :], ALU.add)
                v.drain()
                v.bn_stats(stats[:, h, :], o)
                v.drain()
                v.bn_aggr(mv[:, h, :], stats[:, h, :])
                v.drain().then_inc(s_sdo, 1)
                v.wait_ge(s_sdo2, b + 1)
                r = rstd[:, h:h + 1]
                v.reciprocal(r, r)
                v.drain()
                v.tensor_scalar(o, o, mv[:, h, 0:1], r, ALU.subtract, ALU.mult)
                v.drain()
                v.tensor_tensor(o, o, par[:, 1, :], ALU.mult)
                v.drain()
                v.tensor_tensor(o, o, par[:, 2, :], ALU.add)
                v.drain()
                v.wait_ge(s_x2[h], use)
                v.tensor_tensor(o[0:rows], o[0:rows], xrow[0:rows, h, :], ALU.add)
                v.drain().then_inc(s_x2u, 1)
                v.bn_stats(stats[:, h, :], o)
                v.drain()
                v.bn_aggr(mv[:, h, :], stats[:, h, :])
                v.drain()
                v.tensor_copy(blk(mv2, b), mv[:, h, :])

            with v.Fori(0, (NB - 1) // 2) as i:
                for h in range(2):
                    finish(2 * i + h, h, (i + 1) * 16)
            finish(NB - 1, 0, ((NB - 1) // 2 + 1) * 16, TAIL)
            v.drain().then_inc(s_var, 1)
            v.wait_ge(s_sd, 2)
            v.reciprocal(rstd[:, :], rstd[:, :])
            v.drain()

            normalise(FFN, acc, mv2)
            sort(FFN)
            state(FFN)
            attend(FFN, False)

            fo = facc[:, :, 0:16]
            fd = facc[:, :, 16:20]
            v.tensor_scalar(fd, fd, 1e-16, None, ALU.add)
            v.drain()
            v.reciprocal(fd, fd)
            v.drain()
            v.tensor_tensor(fo.rearrange("p b (h c) -> p b h c", h=FHEADS), fo.rearrange("p b (h c) -> p b h c", h=FHEADS),
                            bc(fd.unsqueeze(3), [P, NB, FHEADS, NE]), ALU.mult)
            v.drain()
            v.tensor_tensor(fo, fo, bc(fpar[:, 0:1, :], [P, NB, 16]), ALU.add)
            v.drain()
            v.tensor_reduce(mv2[:, :, 0], fo, AX.X, ALU.add)
            v.drain()
            v.tensor_scalar(mv2[:, :, 0], mv2[:, :, 0], 1.0 / 16, None, ALU.mult)
            v.drain()
            v.tensor_tensor(fo, fo, bc(mv2[:, :, 0:1], [P, NB, 16]), ALU.subtract)
            v.drain()
            v.tensor_tensor(lnf[:, :, :], fo, fo, ALU.mult)
            v.drain()
            v.tensor_reduce(mv2[:, :, 1], lnf[:, :, :], AX.X, ALU.add)
            v.drain()
            v.tensor_scalar(mv2[:, :, 1], mv2[:, :, 1], 1.0 / 16, None, ALU.mult)
            v.drain().then_inc(s_zf, 1)
            v.wait_ge(s_zf2, 1)
            v.reciprocal(rstd[:, :], rstd[:, :])
            v.drain()
            v.tensor_tensor(fo, fo, bc(rstd[:, :].unsqueeze(2), [P, NB, 16]), ALU.mult)
            v.drain()
            v.tensor_tensor(fo, fo, bc(fpar[:, 1:2, :], [P, NB, 16]), ALU.mult)
            v.drain()
            v.tensor_tensor(fo, fo, bc(fpar[:, 2:3, :], [P, NB, 16]), ALU.add)
            v.drain()
            v.tensor_reduce(sc[:, :, :], fo.rearrange("p b (h e) -> p b e h", h=FHEADS), AX.X, ALU.add)
            v.drain()
            v.tensor_scalar(sc[:, :, :], sc[:, :, :], 1.0 / FHEADS, None, ALU.mult)
            v.memset(cnt[:, :, :], 0.0)
            v.drain()
            for e in range(NE):
                for o in range(NE):
                    if o != e:
                        v.tensor_tensor(cmp[:, :], sc[:, :, o], sc[:, :, e], ALU.is_ge if o < e else ALU.is_gt)
                        v.drain()
                        v.tensor_tensor(cnt[:, :, e], cnt[:, :, e], cmp[:, :], ALU.add)
                        v.drain()
            v.tensor_reduce(cmp[:, :], sc[:, :, :], AX.X, ALU.max)
            v.drain()
            v.tensor_tensor(sc[:, :, :], sc[:, :, :], bc(cmp[:, :].unsqueeze(2), [P, NB, NE]), ALU.subtract)
            v.tensor_scalar(cnt[:, :, :], cnt[:, :, :], 1.5, None, ALU.is_lt)
            v.drain().then_inc(s_zf, 1)
            v.wait_ge(s_zf2, 2)
            v.tensor_tensor(gate[:, :, :], gate[:, :, :], cnt[:, :, :], ALU.mult)
            v.drain()
            v.tensor_reduce(cmp[:, :], gate[:, :, :], AX.X, ALU.add)
            v.drain()
            v.reciprocal(cmp[:, :], cmp[:, :])
            v.drain()
            v.tensor_tensor(gate[:, :, :], gate[:, :, :], bc(cmp[:, :].unsqueeze(2), [P, NB, NE]), ALU.mult)
            v.drain().then_inc(s_gate, 1)

            def add_expert(n, e, b0, nblk):
                for j in range(nblk):
                    o = blk(acc, b0 + j, 0, D)
                    gt = gate[:, bass.ds(b0 + j, 1), e]
                    v.scalar_tensor_tensor(out=o, in0=b2b[:, e, :], scalar=gt, in1=o, op0=ALU.mult, op1=ALU.add)
                v.drain()
                for j in range(nblk):
                    o = blk(acc, b0 + j, 0, D)
                    gt = gate[:, bass.ds(b0 + j, 1), e]
                    if nblk == TOKB:
                        v.wait_ge(s_y, n * TOKB + j + 1)
                    else:
                        v.wait_ge(s_y, (NB // TOKB) * NE * TOKB + e + 1)
                    m = v.scalar_tensor_tensor(out=o, in0=bank[4 + j][:, 0:D], scalar=gt, in1=o, op0=ALU.mult, op1=ALU.add)
                    m.then_inc(s_yu, 1)
                d = v.drain()
                if e == NE - 1:
                    d.then_inc(s_fin, nblk)

            with v.Fori(0, NB // TOKB) as i:
                for e in range(NE):
                    add_expert(i * NE + e, e, i * TOKB, TOKB)
            for e in range(NE):
                add_expert((NB // TOKB) * NE + e, e, (NB // TOKB) * TOKB, 1)


_INS = ["x", "src", "dst", "L0_gnn_W", "L0_gnn_att_src", "L0_gnn_att_dst", "L0_gnn_bias", "L0_gnn_ln_gamma",
        "L0_gnn_ln_beta", "L0_ffn_W_gat", "L0_ffn_att_src", "L0_ffn_att_dst", "L0_ffn_b_gat", "L0_ffn_ln_gamma",
        "L0_ffn_ln_beta", "L0_ffn_W1", "L0_ffn_b1", "L0_ffn_W2", "L0_ffn_b2", "L0_ffn_edge_index"]


def kernel(**inputs):
    import concourse.bacc as bacc
    from concourse.bass_utils import run_bass_kernel_spmd

    nc = bacc.Bacc("TRN2", target_bir_lowering=False, num_devices=1)
    arrays, args = {}, []
    for name in _INS:
        a = np.ascontiguousarray(inputs[name])
        arrays[f"in_{name}"] = a
        args.append(nc.dram_tensor(f"in_{name}", a.shape, mybir.dt.from_np(a.dtype), kind="ExternalInput").ap())
    args.append(nc.dram_tensor("out", (N, D), F32, kind="ExternalOutput").ap())
    build(nc, *args)
    r = run_bass_kernel_spmd(nc, [arrays], core_ids=[0])
    return r.results[0]["out"]
```

```python
from contextlib import ExitStack

import numpy as np

import concourse.bass as bass
from concourse import mybir
from concourse.alu_op_type import AluOpType as ALU

ACT = mybir.ActivationFunctionType
AX = mybir.AxisListType
F32 = mybir.dt.float32
BF16 = mybir.dt.bfloat16
I32 = mybir.dt.int32
U32 = mybir.dt.uint32

P = 128
N = 6250
D = 256
NB = -(-N // P)
TAIL = N - (NB - 1) * P
EPS = 1e-5
SLOPE = 0.2
SENT = NB * P
LOW = -1e30
OUTSIDE = 1 << 27

HALF = 16
GR = 2 * HALF
GR_LOG = 5
OHS = 4
BATCH = 4
NE, FF = 4, 512
FT = FF // P
KT = D // P
FHEADS = 4
CH = 7
NC = NB // CH


HPB = 5


class Graph:

    def __init__(self, name, edges, heads, width):
        self.name, self.edges, self.heads, self.width = name, edges, heads, width
        self.hc = heads * width
        self.row = self.hc + heads
        tiles = -(-edges // P)
        self.tiles = -(-tiles // (OHS * BATCH)) * OHS * BATCH
        self.batches = self.tiles // BATCH
        self.groups = edges // GR + 2 * NB


GNN = Graph("gnn", 100000, 8, 32)
FFN = Graph("ffn", 131072, FHEADS, NE)


def build(nc, x, src, dst, W, att_src, att_dst, bias, gamma, beta, W_gat, fatt_src, fatt_dst, b_gat,
          fgamma, fbeta, W1, b1, W2, b2, edge_index, out):
    ctx = ExitStack()
    with ctx:
        def sb(name, shape, dt=F32):
            return ctx.enter_context(nc.sbuf_tensor(name, shape, dt))

        def sem(name):
            return ctx.enter_context(nc.semaphore(name))

        bank = [ctx.enter_context(nc.psum_tensor(f"bank{i}", [P, 512], F32)) for i in range(8)]

        table = {g.name: nc.dram_tensor(f"table_{g.name}", [SENT + 1, g.row], F32).ap() for g in (GNN, FFN)}
        y_dram = nc.dram_tensor("y_dram", [NB * P, NE * D], F32).ap()
        ell = {g.name: nc.dram_tensor(f"ell_{g.name}", [g.groups * P * GR, 1], U32).ap() for g in (GNN, FFN)}

        acc = sb("acc", [P, NB, GNN.row])
        work = sb("work", [P, NB * D])
        xn_all = work[:, :].rearrange("p (b d) -> p b d", b=NB)
        ring_w = HALF * GNN.row
        ring = {GNN.name: [work[:, s * ring_w:(s + 1) * ring_w].rearrange("p (r w) -> p r w", r=HALF)
                           for s in range(2)]}
        prod_gnn = work[:, 2 * ring_w:2 * ring_w + HALF * GNN.hc].rearrange("p (r w) -> p r w", r=HALF)
        xn2T = work[:, :].rearrange("p (k t) -> p k t", k=KT)
        facc = sb("facc", [P, NB, FFN.row])
        accs = {GNN.name: acc, FFN.name: facc}
        adst = {g.name: sb(f"adst_{g.name}", [P, NB, g.heads]) for g in (GNN, FFN)}
        mrun = {g.name: sb(f"mrun_{g.name}", [P, NB, g.heads]) for g in (GNN, FFN)}
        tmpm = sb("tmpm", [P, NB, 8])

        TM = FFN.tiles
        edge_buf = sb("edge_buf", [P, 5 * TM], I32)
        dst_i, src_i, t_i, lane_slot = (edge_buf[:, i * TM:(i + 1) * TM] for i in range(4))
        t_f = edge_buf[:, 4 * TM:5 * TM].bitcast(F32)
        hh = edge_buf[:, 0:2 * FT * P].bitcast(F32).rearrange("p (s f t) -> p s f t", s=2, f=FT)
        y = edge_buf[:, TM:TM + NE * D].bitcast(F32).rearrange("p (e d) -> p e d", e=NE)
        fring_w = HALF * FFN.row
        fbuf = edge_buf[:, 2 * TM:2 * TM + 2 * fring_w + HALF * FFN.hc].bitcast(F32)
        ring[FFN.name] = [fbuf[:, s * fring_w:(s + 1) * fring_w].rearrange("p (r w) -> p r w", r=HALF) for s in range(2)]
        prod = {GNN.name: prod_gnn, FFN.name: fbuf[:, 2 * fring_w:].rearrange("p (r w) -> p r w", r=HALF)}
        hi_b = sb("hi_b", [P, TM], BF16)
        lo_b = sb("lo_b", [P, TM], BF16)
        OL = sb("OL", [P, OHS, BATCH, P], BF16)
        OH = sb("OH", [P, OHS, BATCH, NB], BF16)
        evenh = sb("evenh", [NB, P])
        Tm = sb("Tm", [P, 2, BATCH, P], BF16)
        OHT = sb("OHT", [NB, 2, BATCH, P])
        Hc = sb("Hc", [NB, BATCH, P])
        junk = sb("junk", [P, BATCH, P])
        rank = sb("rank", [P, BATCH])
        rank_i = sb("rank_i", [P, BATCH], I32)
        q_i = sb("q_i", [P, BATCH], I32)
        b_i = sb("b_i", [P, BATCH], I32)
        addr = sb("addr", [P, 2, BATCH], U32)
        load = sb("load", [P, 2, BATCH], U32)
        sent_i = sb("sent_i", [P, GR], U32)
        ng = sb("ng", [NB, 1])
        ngi = sb("ngi", [NB, 1], I32)
        ngr = sb("ngr", [NB, P])
        cum = {g.name: sb(f"cum_{g.name}", [1, NB + 1], I32) for g in (GNN, FFN)}
        idx = sb("idx", [P, 2, HALF], U32)

        identf = sb("identf", [P, P])
        identb = sb("identb", [P, P], BF16)
        maskb = sb("maskb", [P, P], BF16)
        upper = sb("upper", [NB, NB + 1])
        iota_f = junk[:, 1, :].bitcast(I32)
        iota_b = sb("iota_b", [P, P], BF16)
        zero_b = sb("zero_b", [P, P], BF16)
        eps_t = sb("eps_t", [P, 1])
        sent_row = sb("sent_row", [1, GNN.row + FFN.row])

        xrow2 = sb("xrow", [P, 2, D])
        wx = sb("wx", [P, KT, D + 16])
        fwx = sb("fwx", [P, KT, 16 + 8])
        attb = xrow2[:, :, :]
        fattb = sb("fattb", [P, 2, 16])
        par = sb("par", [P, 3, D])
        fpar = sb("fpar", [P, 3, 16])
        w1 = sb("w1", [P, KT, NE, FF])
        w2 = sb("w2", [P, FT, NE, D])
        b1t = sb("b1t", [P, NE, FT])
        b2b = sb("b2b", [P, NE, D])
        yback = work[:, 0:CH * NE * D].rearrange("p (s e d) -> p s e d", s=CH, e=NE)

        stats = sb("stats", [P, NB, 6])
        mv = sb("mv", [P, NB, 2])
        rstd = sb("rstd", [P, NB])
        mv2 = sb("mv2", [P, NB, 2])
        xT = sb("xT", [P, 2, KT, P])
        xrow = xrow2
        xnrm = sb("xnrm", [P, 2, D])
        zt = sb("zt", [P, HALF, 8])
        ed = sb("ed", [P, 2, (HALF + 1) * 8])
        wt = sb("wt", [P, 2, (HALF + 1) * 8])
        gm = sb("gm", [P, 8])
        mnew = sb("mnew", [P, 8])
        den_p = sb("den_p", [P, 8])
        part_f = sb("part_f", [P, 16])
        sc = tmpm[:, :, :].rearrange("p b h -> p (b h)")[:, 0:NB * NE].rearrange("p (b e) -> p b e", e=NE)
        cnt = tmpm[:, :, :].rearrange("p b h -> p (b h)")[:, NB * NE:2 * NB * NE].rearrange("p (b e) -> p b e", e=NE)
        cmp = sb("cmp", [P, NB])
        gate = sb("gate", [P, NB, NE])
        lnf = t_f[:, 0:NB * 16].rearrange("p (b c) -> p b c", b=NB)

        s_par = sem("s_par")
        s_att = sem("s_att")
        s_norm = sem("s_norm")
        s_xin = sem("s_xin")
        s_xpad = sem("s_xpad")
        s_const = sem("s_const")
        s_cv = sem("s_cv")
        s_wx = sem("s_wx")
        s_var = sem("s_var")
        s_sd = sem("s_sd")
        st = {}
        for g in (GNN, FFN):
            n = g.name
            st[n] = dict(
                xn=sem(f"{n}_xn_ready"),
                tp=sem(f"{n}_xT_in_psum"),
                tc=sem(f"{n}_xT_copied"),
                pj=sem(f"{n}_proj_done"),
                pc=sem(f"{n}_proj_copied"),
                tab=sem(f"{n}_table_written"),
                acc0=sem(f"{n}_state_ready"),
                raw=sem(f"{n}_edges_landed"),
                fill=sem(f"{n}_edge_pad_written"),
                prep=sem(f"{n}_edges_split"),
                oh=sem(f"{n}_onehots_ready"),
                hist=sem(f"{n}_histogram_batch_done"),
                seeded=sem(f"{n}_histogram_seeded"),
                ng=sem(f"{n}_groups_counted"),
                cumr=sem(f"{n}_group_sums_in_psum"),
                cumw=sem(f"{n}_group_sums_ready"),
                pre=sem(f"{n}_ell_prefilled"),
                oh2=sem(f"{n}_rank_onehots_ready"),
                fr=sem(f"{n}_front_in_psum"),
                oht=sem(f"{n}_onehot_T_copied"),
                tm=sem(f"{n}_pairs_ready"),
                hu=sem(f"{n}_running_histogram_updated"),
                hcp=sem(f"{n}_running_histogram_copied"),
                gr=sem(f"{n}_lookup_ready"),
                ranked=sem(f"{n}_ranks_read"),
                ad=sem(f"{n}_slots_ready"),
                seedin=sem(f"{n}_seed_inputs_ready"),
                evn=sem(f"{n}_even_tiles_histogram_copied"),
                sc=[sem(f"{n}_scattered{s}") for s in range(2)],
                ix=[sem(f"{n}_index_landed{s}") for s in range(2)],
                ga=[sem(f"{n}_rows_landed{s}") for s in range(2)],
                ru=[sem(f"{n}_rows_used{s}") for s in range(2)],
                ed=sem(f"{n}_logits_ready"),
                w=sem(f"{n}_weights_ready"),
                pr=sem(f"{n}_products_ready"),
                ps=sem(f"{n}_products_summed"),
                pa=sem(f"{n}_sums_added"),
                end=sem(f"{n}_attended"),
            )
        s_x2 = sem("s_x_landed_again")
        s_sdo = sem("s_out_var_ready")
        s_sdo2 = sem("s_out_sd_ready")
        s_zf = sem("s_gate_exp_in")
        s_zf2 = sem("s_gate_exp_out")
        s_gate = sem("s_gate_ready")
        s_h1 = sem("s_hidden_in_psum")
        s_h1u = sem("s_hidden_activated")
        s_y = sem("s_expert_out_in_psum")
        s_yu = sem("s_expert_out_added")
        s_yr = sem("s_expert_outputs_ready")
        s_ys = sem("s_expert_outputs_stored")
        s_yb = [sem(f"s_expert_outputs_back{i}") for i in range(CH)]
        s_fin = sem("s_chunk_final")
        s_out = sem("s_out_stored")
        s_step = sem("s_pool_step")

        block = ctx.enter_context(nc.Block())

        def bc(ap, shape):
            return ap.to_broadcast(shape)

        @block.sync
        def _(sp):
            sp.sem_inc(s_fin, 1)
            sp.wait_ge(s_xpad, 1)
            sp.dma_start(xn_all[:, 0:NB - 1, :], x[0:(NB - 1) * P, :].rearrange("(b p) d -> p b d", p=P)).then_inc(s_xin, 16)
            sp.dma_start(xn_all[0:TAIL, NB - 1, :], x[(NB - 1) * P:N, :]).then_inc(s_xin, 16)
            sp.dma_start(wx[:, :, 0:D], W.rearrange("(k p) n -> p k n", p=P)).then_inc(s_att, 16)
            sp.dma_start(attb[:, 0, :], att_src.rearrange("(a h) c -> a (h c)", a=1).to_broadcast([P, D])).then_inc(s_att, 16)
            sp.dma_start(attb[:, 1, :], att_dst.rearrange("(a h) c -> a (h c)", a=1).to_broadcast([P, D])).then_inc(s_att, 16)
            sp.dma_start(fwx[:, :, 0:16], W_gat.rearrange("(k p) n -> p k n", p=P)).then_inc(s_att, 16)
            sp.dma_start(fattb[:, 0, :], fatt_src.rearrange("(a h) c -> a (h c)", a=1).to_broadcast([P, 16])).then_inc(s_att, 16)
            sp.dma_start(fattb[:, 1, :], fatt_dst.rearrange("(a h) c -> a (h c)", a=1).to_broadcast([P, 16])).then_inc(s_att, 16)
            raw = st["gnn"]["raw"]
            T = GNN.tiles
            full = GNN.edges // T
            rest = GNN.edges - full * T
            sp.wait_ge(st["gnn"]["fill"], 1)
            for to, of in ((dst_i, dst), (src_i, src)):
                sp.dma_start(to[0:full, 0:T], of[0:full * T].rearrange("(p t) -> p t", t=T)).then_inc(raw, 16)
                sp.dma_start(to[full:full + 1, 0:rest], of[full * T:GNN.edges].rearrange("(p t) -> p t", p=1)).then_inc(raw, 16)
            for i, v in enumerate((bias, gamma, beta)):
                sp.dma_start(par[:, i, :], v.rearrange("(a d) -> a d", a=1).to_broadcast([P, D])).then_inc(s_norm, 16)
            for i, v in enumerate((b_gat, fgamma, fbeta)):
                sp.dma_start(fpar[:, i, :], v.rearrange("(a d) -> a d", a=1).to_broadcast([P, 16])).then_inc(s_norm, 16)
            for e in range(NE):
                sp.dma_start(w1[:, :, e, :], W1[e].rearrange("(k p) f -> p k f", p=P)).then_inc(s_par, 16)
                sp.dma_start(w2[:, :, e, :], W2[e].rearrange("(f p) d -> p f d", p=P)).then_inc(s_par, 16)
                sp.dma_start(b2b[:, e, :], b2[e:e + 1, :].to_broadcast([P, D])).then_inc(s_par, 16)
            with nc.allow_non_contiguous_dma(reason="b1 by hidden unit on the partitions"):
                sp.dma_start(b1t[:, :, :], b1.rearrange("e (f p) -> p e f", p=P)).then_inc(s_par, 16)

            def tables(g, off):
                s = st[g.name]
                sp.wait_ge(s["pc"], NB)
                sp.dma_start(table[g.name][0:SENT, :].rearrange("(b p) w -> p b w", p=P), accs[g.name][:, :, :]).then_inc(s["tab"], 16)
                sp.dma_start(table[g.name][SENT:SENT + 1, :], sent_row[:, off:off + g.row]).then_inc(s["tab"], 16)

            def prefill(g):
                s = st[g.name]
                sp.wait_ge(s["cumw"], 1)
                total = sp.value_load(cum[g.name][0:1, NB:NB + 1], min_val=NB, max_val=g.groups)
                with sp.Fori(0, total) as i:
                    sp.dma_start(ell[g.name][bass.ds(i * (P * GR), P * GR), :].rearrange("(p r) o -> p (r o)", p=P),
                                 sent_i[:, :]).then_inc(s["pre"], 16)
                sp.wait_ge(s["pre"], total * 16)
                sp.sem_inc(s["cumw"], 1)

            def indices(g, store_y=False):
                s = st[g.name]
                for h in range(2):
                    sp.wait_ge(s["sc"][h], 16 * BATCH * (g.batches // 2))
                with sp.Fori(0, NB) as b:
                    first = sp.value_load(cum[g.name][0:1, bass.ds(b, 1)], min_val=0, max_val=g.groups - 1)
                    last = sp.value_load(cum[g.name][0:1, bass.ds(b + 1, 1)], min_val=1, max_val=g.groups)
                    with sp.Fori(first, last) as i:
                        index_pair(g, s, i)
                    if store_y:
                        sp.wait_ge(s_yr, b + 1)
                        sp.dma_start(y_dram[bass.ds(b * P, P), :], y.rearrange("p e d -> p (e d)")).then_inc(s_ys, 16)

            def index_pair(g, s, i):
                    for h in range(2):
                        sp.wait_ge(s["ru"][h], i + 1)
                        sp.dma_start(idx[:, h, :], ell[g.name][bass.ds(i * (P * GR), P * GR), :].rearrange("(p r) o -> p (r o)", p=P)[:, h * HALF:(h + 1) * HALF]).then_inc(s["ix"][h], 16)

            sp.wait_ge(s_cv, 1)
            sp.wait_ge(s_const, 1)
            prefill(GNN)
            tables(GNN, 0)
            sp.wait_ge(st["gnn"]["sc"][0], 16 * BATCH * (GNN.batches // 2))
            sp.wait_ge(st["gnn"]["sc"][1], 16 * BATCH * (GNN.batches // 2))
            T = FFN.tiles
            sp.dma_start(dst_i, edge_index[1].rearrange("(p t) -> p t", t=T)).then_inc(st["ffn"]["raw"], 16)
            sp.dma_start(src_i, edge_index[0].rearrange("(p t) -> p t", t=T)).then_inc(st["ffn"]["raw"], 16)
            indices(GNN)
            sp.wait_ge(st["gnn"]["end"], 1)
            sp.dma_start(xn_all[:, 0:NB - 1, :], x[0:(NB - 1) * P, :].rearrange("(b p) d -> p b d", p=P)).then_inc(s_x2, 16)
            sp.dma_start(xn_all[0:TAIL, NB - 1, :], x[(NB - 1) * P:N, :]).then_inc(s_x2, 16)
            prefill(FFN)
            tables(FFN, GNN.row)
            indices(FFN, store_y=True)
            sp.wait_ge(s_ys, 16 * NB + 16)
            sp.wait_ge(s_gate, 1)
            with sp.Fori(0, NC) as c:
                for j in range(CH):
                    sp.wait_ge(s_fin, c + 1)
                    sp.dma_start(yback[:, j].rearrange("p e d -> p (e d)"), y_dram[bass.ds((c * CH + j) * P, P), :]).then_inc(s_yb[j], 16)
            sp.wait_ge(s_out, 16 * (NC + 1))

        @block.gpsimd
        def _(pool):
            pool.memset(identf[:, :], 0.0)
            pool.memset(upper[:, :], 1.0)
            pool.memset(sent_row[:, :], 0.0)
            pool.drain()
            pool.memset(sent_row[0:1, GNN.hc:GNN.row], LOW)
            pool.memset(sent_row[0:1, GNN.row + FFN.hc:GNN.row + FFN.row], LOW)
            pool.iota(iota_f[:, :], pattern=[[1, P]], base=0, channel_multiplier=0)
            pool.iota(sent_i[:, :], pattern=[[0, GR]], base=SENT, channel_multiplier=0)
            pool.affine_select(out=identf[:, :], in_=identf[:, :], compare_op=ALU.not_equal, fill=1.0,
                               base=0, pattern=[[-1, P]], channel_multiplier=1)
            pool.affine_select(out=upper[:, :], in_=upper[:, :], compare_op=ALU.is_gt, fill=0.0,
                               base=0, pattern=[[1, NB + 1]], channel_multiplier=-1)
            pool.memset(junk[:, 0, :], float(1 << 20))
            pool.drain()
            pool.affine_select(out=junk[:, 0, :], in_=junk[:, 0, :], compare_op=ALU.is_ge, fill=0.0,
                               base=0, pattern=[[-1, P]], channel_multiplier=1)
            pool.drain().then_inc(s_const, 1)

            def scatters(g):
                s = st[g.name]
                pool.wait_ge(s["cumw"], 2)
                with pool.Fori(0, g.batches // 2) as i:
                    for h in range(2):
                        pool.wait_ge(s["ad"], 2 * i + h + 1)
                        pool.sem_inc(s_step, 1)
                        for k in range(BATCH):
                            pool.indirect_dma_start(ell[g.name], bass.IndirectOffsetOnAxis(addr[:, h, k:k + 1], 0),
                                                    load[:, h, k:k + 1], None, bounds_check=g.groups * P * GR - 1,
                                                    oob_is_err=False).then_inc(s["sc"][h], 16)

            def gathers(g):
                s = st[g.name]
                for h in range(2):
                    pool.sem_inc(s["ru"][h], 1)
                pool.wait_ge(s["acc0"], 1)
                pool.wait_ge(s["tab"], 32)
                pool.wait_ge(s["cumw"], 1)
                total = pool.value_load(cum[g.name][0:1, NB:NB + 1], min_val=NB, max_val=g.groups)
                with pool.Fori(0, total) as i:
                    for h in range(2):
                        pool.wait_ge(s["ix"][h], (i + 1) * 16)
                        pool.wait_ge(s["ru"][h], i + 1)
                        pool.sem_inc(s_step, 1)
                        for r in range(HALF):
                            pool.indirect_dma_start(ring[g.name][h][:, r, :], None, table[g.name],
                                                    bass.IndirectOffsetOnAxis(idx[:, h, r:r + 1], 0)).then_inc(s["ga"][h], 16)

            scatters(GNN)
            gathers(GNN)
            scatters(FFN)
            gathers(FFN)

        @block.scalar
        def _(act):
            def proj(g, stage):
                s = st[g.name]
                act.wait_ge(s_var, stage)
                act.activation(rstd[:, :], (mv if stage == 1 else mv2)[:, :, 1], ACT.Sqrt, bias=eps_t[:, 0:1]).then_inc(s_sd, 1)
                def copy(b, h):
                    act.wait_ge(s["tp"], b + 1)
                    if not isinstance(b, int) or b >= 2:
                        act.wait_ge(s["pj"], b - 1)
                    rows_t = bank[h][:, 0:D].rearrange("p (k t) -> p k t", k=KT)
                    if stage == 2:
                        act.activation(xn2T[:, :, bass.ds(b * P, P)], rows_t, ACT.Copy)
                    act.activation(xT[:, h], rows_t, ACT.Copy).then_inc(s["tc"], 1)
                copy(0, 0)
                copy(1, 1)
                with act.Fori(1, (NB - 1) // 2) as i:
                    for h in range(2):
                        copy(2 * i + h, h)
                copy(NB - 1, 0)

            def ranks(g):
                s = st[g.name]
                act.wait_ge(s["seeded"], 1)
                for c in range(2):
                    act.activation(Hc[:, c, :], bank[c][0:NB, 0:P], ACT.Copy).then_inc(s["hcp"], 1)

                def onehot(n, h):
                    act.wait_ge(s["fr"], n + 1)
                    act.activation(OHT[:, h], bank[6 + h][0:NB, 0:BATCH * P // 2].bitcast(BF16).rearrange("p (k e) -> p k e", k=BATCH), ACT.Copy).then_inc(s["oht"], 1)

                def chain(n):
                    for k in range(BATCH):
                        act.wait_ge(s["hu"], n * BATCH + k + 1)
                        act.activation(Hc[:, (k + 2) % BATCH, :], bank[k % 2][0:NB, 0:P], ACT.Copy).then_inc(s["hcp"], 1)

                onehot(0, 0)
                with act.Fori(0, g.batches // 2 - 1) as i:
                    for h in range(2):
                        onehot(2 * i + h + 1, 1 - h)
                        chain(2 * i + h)
                onehot(g.batches - 1, 1)
                chain(g.batches - 2)
                chain(g.batches - 1)

            def weights(g, experts=False):
                s = st[g.name]
                w = (HALF + 1) * g.heads
                with act.Fori(0, NB) as b:
                    if experts:
                        hidden(b)
                    first = act.value_load(cum[g.name][0:1, bass.ds(b, 1)], min_val=0, max_val=g.groups - 1)
                    last = act.value_load(cum[g.name][0:1, bass.ds(b + 1, 1)], min_val=1, max_val=g.groups)
                    with act.Fori(first, last) as i:
                        for h in range(2):
                            act.wait_ge(s["ed"], 2 * i + h + 1)
                            act.activation(wt[:, h, 0:w], ed[:, h, 0:w], ACT.Exp).then_inc(s["w"], 1)

            def hidden(b):
                for e in range(NE):
                    act.wait_ge(s_h1, b * NE + e + 1)
                    act.wait_ge(s_y, b * NE + e + 1)
                    for f in range(FT):
                        m = act.activation(hh[:, e % 2, f, :], bank[e % 2][:, f * P:(f + 1) * P], ACT.Gelu, bias=b1t[:, e, f:f + 1])
                    m.then_inc(s_h1u, 1)

            act.wait_ge(s_cv, 1)
            proj(GNN, 1)
            ranks(GNN)
            weights(GNN)
            with act.Fori(0, NC) as c:
                act.wait_ge(s_sdo, c + 1)
                act.activation(rstd[:, 0:CH], mv[:, 0:CH, 1], ACT.Sqrt, bias=eps_t[:, 0:1]).then_inc(s_sdo2, 1)
            proj(FFN, 2)
            ranks(FFN)
            act.wait_ge(s_par, 16 * (3 * NE + 1))
            act.sem_inc(s_h1u, 2)
            act.sem_inc(s_y, 2)
            for h in range(2):
                act.wait_ge(st["ffn"]["sc"][h], 16 * BATCH * (FFN.batches // 2))
            weights(FFN, experts=True)
            act.wait_ge(s_zf, 1)
            act.activation(rstd[:, :], mv2[:, :, 1], ACT.Sqrt, bias=eps_t[:, 0:1]).then_inc(s_zf2, 1)
            act.wait_ge(s_zf, 2)
            act.activation(gate[:, :, :], sc, ACT.Exp).then_inc(s_zf2, 1)
            with act.Fori(0, NC - 1) as c:
                act.wait_ge(s_fin, c + 2)
                act.dma_start(out[bass.ds(c * (CH * P), CH * P), :].rearrange("(b p) d -> p b d", p=P), acc[:, bass.ds(c * CH, CH), 0:D]).then_inc(s_out, 16)
            act.wait_ge(s_fin, NC + 1)
            act.dma_start(out[(NC - 1) * CH * P:(NB - 1) * P, :].rearrange("(b p) d -> p b d", p=P), acc[:, (NC - 1) * CH:NB - 1, 0:D]).then_inc(s_out, 16)
            act.dma_start(out[(NB - 1) * P:N, :], acc[0:TAIL, NB - 1, 0:D]).then_inc(s_out, 16)

        @block.tensor
        def _(pe):
            def proj(g, stage):
                s = st[g.name]
                ncol = g.row + g.heads
                wgt = wx if stage == 1 else fwx

                def block_of(b, h):
                    pe.wait_ge(s["xn"], b + 1)
                    if not isinstance(b, int) or b >= 2:
                        pe.wait_ge(s["tc"], b - 1)
                        pe.wait_ge(s["pc"], b - 1)
                    for k in range(KT):
                        t = pe.transpose(bank[h][:, k * P:(k + 1) * P], xnrm[:, h, k * P:(k + 1) * P], identf[:, :])
                    t.then_inc(s["tp"], 1)
                    pe.wait_ge(s["tc"], b + 1)
                    for k in range(KT):
                        m = pe.matmul(bank[2 + h][:, 0:ncol], xT[:, h, k, :], wgt[:, k, 0:ncol], start=(k == 0), stop=(k == KT - 1))
                    m.then_inc(s["pj"], 1)

                block_of(0, 0)
                block_of(1, 1)
                with pe.Fori(1, (NB - 1) // 2) as i:
                    for h in range(2):
                        block_of(2 * i + h, h)
                block_of(NB - 1, 0)

            def start_histogram():
                for c in range(2):
                    pe.matmul(bank[c][0:NB, 0:P], zero_b[:, 0:NB], zero_b[:, :], start=True, stop=False, skip_group_check=True)

            def histogram(g, n, h):
                s = st[g.name]
                pe.wait_ge(s["oh"], n + 1)
                for k in range(BATCH):
                    m = pe.matmul(bank[k % 2][0:NB, 0:P], OH[:, h, k, :], OL[:, h, k, :], start=False, stop=False, skip_group_check=True)
                m.then_inc(s["hist"], 1)

            def end_histogram(g):
                s = st[g.name]
                pe.wait_ge(s["ng"], 1)
                pe.matmul(bank[2][0:1, 0:NB + 1], ng[:, 0:1], upper[:, :], start=True, stop=True).then_inc(s["cumr"], 1)

            def ranks(g):
                s = st[g.name]
                pe.wait_ge(s["seedin"], 1)
                pe.matmul(bank[0][0:NB, 0:P], upper[:, 0:NB], ngr[:, :], start=True, stop=False, skip_group_check=True)
                pe.matmul(bank[1][0:NB, 0:P], upper[:, 0:NB], ngr[:, :], start=True, stop=False, skip_group_check=True)
                pe.matmul(bank[1][0:NB, 0:P], identf[0:NB, 0:NB], evenh[:, :], start=False, stop=False, skip_group_check=True).then_inc(s["seeded"], 1)

                def front(n, o, h):
                    pe.wait_ge(s["oh2"], n + 1)
                    if not isinstance(n, int) or n >= 2:
                        pe.wait_ge(s["tm"], n)
                        pe.wait_ge(s["oht"], n)
                    for k in range(BATCH):
                        pe.matmul(bank[4 + h][:, k * P:(k + 1) * P], bc(hi_b[:, bass.ds(n * BATCH + k, 1)], [P, P]), identb[:, :],
                                  start=True, stop=False, skip_group_check=True)
                        pe.matmul(bank[4 + h][:, k * P:(k + 1) * P], identb[:, :], maskb[:, :], start=False, stop=True, skip_group_check=True)
                    for k in range(BATCH):
                        t = pe.transpose(bank[6 + h][0:NB, k * P // 2:(k + 1) * P // 2].bitcast(BF16), OH[:, o, k, :], identb[:, :])
                    t.then_inc(s["fr"], 1)

                def chain(n, o, h):
                    pe.wait_ge(s["oht"], n + 2)
                    pe.wait_ge(s["tm"], n + 2)
                    pe.wait_ge(s["ranked"], n + 1)
                    for k in range(BATCH):
                        col = slice(k * P, (k + 1) * P)
                        pe.matmul(bank[2 + h][:, col], Tm[:, h, k, :], OL[:, o, k, :], start=True, stop=False, skip_group_check=True)
                        pe.wait_ge(s["hcp"], n * BATCH + k + 1)
                        m = pe.matmul(bank[2 + h][:, col], OHT[:, h, k, :], Hc[:, k, :], start=False, stop=True, skip_group_check=True)
                        if k == BATCH - 1:
                            m.then_inc(s["gr"], 1)
                        pe.matmul(bank[k % 2][0:NB, 0:P], OH[:, o, k, :], OL[:, o, k, :], start=False, stop=False, skip_group_check=True).then_inc(s["hu"], 1)

                pe.sem_inc(s["tm"], 1)
                pe.sem_inc(s["oht"], 1)
                front(0, 0, 0)
                with pe.Fori(0, g.batches // OHS - 1) as i:
                    for j in range(OHS):
                        front(OHS * i + j + 1, (j + 1) % OHS, (j + 1) % 2)
                        chain(OHS * i + j, j, j % 2)
                for j in range(OHS):
                    n = g.batches - OHS + j
                    if j < OHS - 1:
                        front(n + 1, j + 1, (j + 1) % 2)
                    chain(n, j, j % 2)

            def sums(g, per_block):
                s = st[g.name]
                with pe.Fori(0, NB) as b:
                    per_block(b)
                    first = pe.value_load(cum[g.name][0:1, bass.ds(b, 1)], min_val=0, max_val=g.groups - 1)
                    last = pe.value_load(cum[g.name][0:1, bass.ds(b + 1, 1)], min_val=1, max_val=g.groups)
                    with pe.Fori(first, last) as i:
                        for h in range(2):
                            pe.wait_ge(s["pr"], 2 * i + h + 1)
                            pe.wait_ge(s["pa"], 2 * i + h + 1)
                            for r in range(HALF):
                                m = pe.matmul(bank[4 + h][:, 0:g.hc], identf[:, :], prod[g.name][:, r, :], start=(r == 0), stop=(r == HALF - 1))
                            m.then_inc(s["ps"], 1)

            def experts(b):
                def first(e):
                    pe.wait_ge(s_h1u, b * NE + e + 1)
                    for f in range(FT):
                        for k in range(KT):
                            m = pe.matmul(bank[e % 2][:, f * P:(f + 1) * P], w1[:, k, e, f * P:(f + 1) * P], xn2T[:, k, bass.ds(b * P, P)],
                                          start=(k == 0), stop=(k == KT - 1), skip_group_check=True)
                    m.then_inc(s_h1, 1)

                def second(e):
                    pe.wait_ge(s_h1u, b * NE + e + 3)
                    pe.wait_ge(s_yu, b * NE + e + 1)
                    for f in range(FT):
                        m = pe.matmul(bank[2 + e % 2][:, 0:D], hh[:, e % 2, f, :], w2[:, f, e, :], start=(f == 0), stop=(f == FT - 1))
                    m.then_inc(s_y, 1)

                first(0)
                for e in range(1, NE):
                    first(e)
                    second(e - 1)
                second(NE - 1)

            pe.wait_ge(s_const, 1)
            pe.wait_ge(s_cv, 2)
            start_histogram()
            with pe.Fori(0, GNN.batches // 2) as i:
                for h in range(2):
                    histogram(GNN, 2 * i + h, h)
            end_histogram(GNN)
            pe.wait_ge(st["gnn"]["cumw"], 1)
            pe.wait_ge(s_wx, 1)
            proj(GNN, 1)
            pe.wait_ge(st["gnn"]["pc"], NB)
            ranks(GNN)
            pe.wait_ge(st["gnn"]["hcp"], GNN.tiles + 2)
            start_histogram()

            def next_histogram(b):
                for j in range(HPB):
                    histogram(FFN, b * HPB + j, j % 2)

            sums(GNN, next_histogram)
            for j in range(FFN.batches - NB * HPB):
                histogram(FFN, NB * HPB + j, j % 2)
            end_histogram(FFN)
            pe.wait_ge(st["ffn"]["cumw"], 1)
            proj(FFN, 2)
            pe.wait_ge(st["ffn"]["pc"], NB)
            ranks(FFN)
            pe.wait_ge(st["ffn"]["hcp"], FFN.tiles + 2)
            pe.wait_ge(st["ffn"]["ranked"], FFN.batches + 2)
            pe.wait_ge(s_par, 16 * (3 * NE + 1))
            with pe.Fori(0, NB) as b:
                experts(b)

        @block.vector
        def _(v):
            v.memset(xn_all[:, NB - 1, :], 0.0)
            v.drain().then_inc(s_xpad, 1)
            v.memset(dst_i[:, :], -1)
            v.memset(src_i[:, :], 0)
            v.drain().then_inc(st["gnn"]["fill"], 1)
            v.memset(eps_t[:, :], EPS)
            v.memset(zero_b[:, :], 0.0)
            v.drain().then_inc(s_cv, 1)
            v.wait_ge(s_const, 1)
            v.tensor_copy(iota_b[:, :], iota_f[:, :])
            v.tensor_copy(identb[:, :], identf[:, :])
            v.tensor_copy(maskb[:, :], junk[:, 0, :])
            v.drain().then_inc(s_cv, 1)
            v.wait_ge(s_att, 16 * 6)
            tmpw = t_f[:, 0:D]
            for (wgt, at, g) in ((wx, attb, GNN), (fwx, fattb, FFN)):
                for k in range(KT):
                    for a in range(2):
                        v.tensor_tensor(tmpw[:, 0:g.hc], wgt[:, k, 0:g.hc], at[:, a, :], ALU.mult)
                        v.drain()
                        v.tensor_reduce(wgt[:, k, g.hc + a * g.heads:g.hc + (a + 1) * g.heads],
                                        tmpw[:, 0:g.hc].rearrange("p (h c) -> p h c", c=g.width), AX.X, ALU.add)
                        v.drain()
            v.drain().then_inc(s_wx, 1)

            def mean_var(of, b):
                v.bn_stats(stats[:, bass.ds(b, 1), :].rearrange("p a s -> p (a s)"), of)

            def blk(t, b, lo=0, hi=None):
                return t[:, bass.ds(b, 1), lo:hi if hi is not None else t.shape[2]].rearrange("p a d -> p (a d)")

            def state(g):
                s = st[g.name]
                a = accs[g.name]
                v.wait_ge(s["tab"], 32)
                tm = tmpm[:, :, 0:g.heads]
                v.tensor_tensor(tm, a[:, :, g.hc:g.row], adst[g.name][:, :, :], ALU.add)
                v.drain()
                v.scalar_tensor_tensor(out=mrun[g.name][:, :, :], in0=tm, scalar=SLOPE, in1=tm, op0=ALU.mult, op1=ALU.max)
                v.memset(a[:, :, g.hc:g.row], 1.0)
                v.drain().then_inc(s["acc0"], 1)

            def proj_out(g, b, h):
                s = st[g.name]
                v.wait_ge(s["pj"], b + 1)
                v.tensor_copy(blk(accs[g.name], b), bank[2 + h][:, 0:g.row])
                v.tensor_copy(blk(adst[g.name], b), bank[2 + h][:, g.row:g.row + g.heads])
                v.drain().then_inc(s["pc"], 1)

            def normalise(g, of, mean):
                s = st[g.name]

                def norm(b, h):
                    if not isinstance(b, int) or b >= 2:
                        v.wait_ge(s["tp"], b - 1)
                    v.tensor_scalar(xnrm[:, h, :], blk(of, b, 0, D), blk(mean, b, 0, 1), rstd[:, bass.ds(b, 1)], ALU.subtract, ALU.mult)
                    v.drain().then_inc(s["xn"], 1)

                norm(0, 0)
                norm(1, 1)
                proj_out(g, 0, 0)
                with v.Fori(1, (NB - 1) // 2) as i:
                    for h in range(2):
                        norm(2 * i + h, h)
                        proj_out(g, 2 * i + h - 1, 1 - h)
                norm(NB - 1, 0)
                proj_out(g, NB - 2, 1)
                proj_out(g, NB - 1, 0)

            def split_edges(g):
                s = st[g.name]
                T = g.tiles
                v.wait_ge(s["raw"], 64 if g is GNN else 32)
                di, si, ti, tf = dst_i[:, 0:T], src_i[:, 0:T], t_i[:, 0:T], t_f[:, 0:T]
                v.tensor_scalar(ti, di, 7, None, ALU.logical_shift_right)
                v.tensor_scalar(di, di, P - 1, None, ALU.bitwise_and)
                v.tensor_scalar(tf, si, 0.0, float(N), ALU.is_lt, ALU.mult)
                v.drain()
                v.tensor_copy(hi_b[:, 0:T], ti)
                v.tensor_copy(lo_b[:, 0:T], di)
                v.tensor_tensor(tf, si, tf, ALU.add)
                v.tensor_scalar(lane_slot[:, 0:T], ti, float(NB), float(OUTSIDE), ALU.is_ge, ALU.mult)
                v.drain()
                v.tensor_scalar(si, tf, 0.0, float(N - 1), ALU.max, ALU.min)
                v.tensor_scalar(ti, di, GR_LOG, None, ALU.logical_shift_left)
                v.drain()
                v.tensor_tensor(lane_slot[:, 0:T], lane_slot[:, 0:T], ti, ALU.bitwise_or)
                v.drain()

            def onehots(n, o):
                v.tensor_tensor(OL[:, o], bc(iota_b[:, 0:P].unsqueeze(1), [P, BATCH, P]),
                                bc(lo_b[:, bass.ds(n * BATCH, BATCH)].unsqueeze(2), [P, BATCH, P]), ALU.is_equal)
                return v.tensor_tensor(OH[:, o], bc(iota_b[:, 0:NB].unsqueeze(1), [P, BATCH, NB]),
                                       bc(hi_b[:, bass.ds(n * BATCH, BATCH)].unsqueeze(2), [P, BATCH, NB]), ALU.is_equal)

            def histogram(g, n, o, alone=False):
                v.wait_ge(st[g.name]["hist"], n + 1 if alone else n)
                onehots(n, o).then_inc(st[g.name]["oh"], 1)

            def count_groups(g):
                s = st[g.name]
                v.wait_ge(s["hist"], g.batches + 1)
                v.tensor_copy(evenh[:, :], bank[0][0:NB, 0:P])
                v.drain()
                v.tensor_tensor(ngr[:, :], evenh[:, :], bank[1][0:NB, 0:P], ALU.add)
                v.drain()
                v.tensor_reduce(ng[:, :], ngr[:, :], AX.X, ALU.max)
                v.drain()
                v.tensor_scalar(ngi[:, :], ng[:, :], 1.0, float(GR - 1), ALU.max, ALU.add)
                v.drain()
                v.tensor_scalar(ngi[:, :], ngi[:, :], GR_LOG, None, ALU.logical_shift_right)
                v.drain()
                v.tensor_copy(ng[:, :], ngi[:, :]).then_inc(s["ng"], 1)
                v.drain()
                v.tensor_scalar(ngr[:, :], bc(ng[:, :], [NB, P]), float(GR), None, ALU.mult).then_inc(s["seedin"], 1)
                v.wait_ge(s["cumr"], 1)
                v.tensor_copy(cum[g.name][:, :], bank[2][0:1, 0:NB + 1]).then_inc(s["cumw"], 1)

            def ranks(g):
                s = st[g.name]
                v.engine_nop().then_inc(s["ranked"], 2)

                def first_half(n, o):
                    onehots(n, o).then_inc(s["oh2"], 1)

                def pairs(n, h):
                    v.wait_ge(s["fr"], n + 1)
                    return v.tensor_tensor(Tm[:, h], bank[4 + h][:, :].rearrange("p (k e) -> p k e", k=BATCH),
                                           bc(hi_b[:, bass.ds(n * BATCH, BATCH)].unsqueeze(2), [P, BATCH, P]), ALU.is_equal).then_inc(s["tm"], 1)

                def look_up(n, o, h):
                    v.wait_ge(s["gr"], n + 1)
                    for k in range(BATCH):
                        m = v.scalar_tensor_tensor(out=junk[:, k, :], in0=bank[2 + h][:, k * P:(k + 1) * P], scalar=1.0,
                                                   in1=OL[:, o, k, :], op0=ALU.mult, op1=ALU.mult, accum_out=rank[:, k:k + 1])
                    m.then_inc(s["ranked"], 1)

                def slots(n, h, use, filler=None):
                    v.drain()
                    v.tensor_copy(rank_i[:, :], rank[:, :])
                    if filler:
                        filler()
                    v.drain()
                    if not isinstance(use, int) or use > 0:
                        v.wait_ge(s["sc"][h], use * (16 * BATCH))
                    v.tensor_scalar(q_i[:, :], rank_i[:, :], GR_LOG, GR_LOG + 7, ALU.logical_shift_right, ALU.logical_shift_left)
                    v.scalar_tensor_tensor(out=b_i[:, :], in0=rank_i[:, :], scalar=GR - 1,
                                           in1=lane_slot[:, bass.ds(n * BATCH, BATCH)], op0=ALU.bitwise_and, op1=ALU.bitwise_or)
                    v.tensor_copy(load[:, h, :], src_i[:, bass.ds(n * BATCH, BATCH)])
                    v.drain()
                    v.tensor_tensor(addr[:, h, :], q_i[:, :].bitcast(U32), b_i[:, :].bitcast(U32), ALU.bitwise_or).then_inc(s["ad"], 1)

                def step(i, j, ahead=True, behind=True):
                    n = OHS * i + j
                    if ahead:
                        first_half(n + 3, (j + 3) % OHS)
                    look_up(n, j, j % 2)
                    slots(n, j % 2, 2 * i + j // 2, (lambda: pairs(n + 2, j % 2)) if behind else None)

                for n in range(3):
                    first_half(n, n)
                    if n > 0:
                        pairs(n - 1, n - 1)
                for j in range(OHS):
                    step(0, j)
                last = g.batches // OHS - 1
                with v.Fori(1, last) as i:
                    for j in range(OHS):
                        step(i, j)
                for j in range(OHS):
                    step(last, j, ahead=j == 0, behind=j < 2)

            def attend(g, on_pe, per_block=None):
                s = st[g.name]
                H, C, HC = g.heads, g.width, g.hc
                a, m = accs[g.name], mrun[g.name]
                pr = prod[g.name]
                z = zt[:, :, 0:H]
                if on_pe:
                    v.sem_inc(s["ps"], 1)
                    v.sem_inc(s["pa"], 2)
                with v.Fori(0, NB) as b:
                    if per_block:
                        per_block(b)
                    first = v.value_load(cum[g.name][0:1, bass.ds(b, 1)], min_val=0, max_val=g.groups - 1)
                    last = v.value_load(cum[g.name][0:1, bass.ds(b + 1, 1)], min_val=1, max_val=g.groups)
                    with v.Fori(first, last) as i:
                        for h in range(2):
                            rows = ring[g.name][h]
                            e_ = ed[:, h, 0:HALF * H].rearrange("p (r h) -> p r h", r=HALF)
                            w_ = wt[:, h, 0:HALF * H].rearrange("p (r h) -> p r h", r=HALF)
                            old = ed[:, h, HALF * H:(HALF + 1) * H]
                            sc_ = wt[:, h, HALF * H:(HALF + 1) * H]
                            v.wait_ge(s["ga"][h], (i + 1) * (16 * HALF))
                            v.tensor_tensor(z, rows[:, :, HC:HC + H], bc(blk(adst[g.name], b).unsqueeze(1), [P, HALF, H]), ALU.add)
                            v.drain()
                            v.scalar_tensor_tensor(out=e_, in0=z, scalar=SLOPE, in1=z, op0=ALU.mult, op1=ALU.max)
                            v.drain()
                            v.tensor_reduce(gm[:, 0:H], e_.rearrange("p r h -> p h r"), AX.X, ALU.max)
                            v.drain()
                            v.tensor_tensor(mnew[:, 0:H], gm[:, 0:H], blk(m, b), ALU.max)
                            v.drain()
                            v.tensor_tensor(e_, e_, bc(mnew[:, 0:H].unsqueeze(1), [P, HALF, H]), ALU.subtract)
                            v.tensor_tensor(old, blk(m, b), mnew[:, 0:H], ALU.subtract).then_inc(s["ed"], 1)
                            v.wait_ge(s["w"], 2 * i + h + 1)
                            if on_pe:
                                v.wait_ge(s["ps"], 2 * i + h + 1)
                            p_ = v.tensor_tensor(pr.rearrange("p r (h c) -> p r h c", c=C),
                                                 rows[:, :, 0:HC].rearrange("p r (h c) -> p r h c", c=C),
                                                 bc(w_.unsqueeze(3), [P, HALF, H, C]), ALU.mult)
                            if on_pe:
                                p_.then_inc(s["pr"], 1)
                            v.tensor_reduce(den_p[:, 0:H], w_.rearrange("p r h -> p h r"), AX.X, ALU.add).then_inc(s["ru"][h], 1)
                            v.tensor_tensor(blk(a, b, 0, HC).rearrange("p (h c) -> p h c", c=C),
                                            blk(a, b, 0, HC).rearrange("p (h c) -> p h c", c=C),
                                            bc(sc_.unsqueeze(2), [P, H, C]), ALU.mult)
                            v.tensor_tensor(blk(a, b, HC, HC + H), blk(a, b, HC, HC + H), sc_, ALU.mult)
                            if not on_pe:
                                v.drain()
                                v.tensor_reduce(part_f[:, 0:HC], pr.rearrange("p r w -> p w r"), AX.X, ALU.add)
                            v.drain()
                            v.tensor_copy(blk(m, b), mnew[:, 0:H])
                            v.tensor_tensor(blk(a, b, HC, HC + H), blk(a, b, HC, HC + H), den_p[:, 0:H], ALU.add)
                            if on_pe:
                                v.wait_ge(s["ps"], 2 * i + h + 2)
                                v.tensor_tensor(blk(a, b, 0, HC), blk(a, b, 0, HC), bank[4 + h][:, 0:HC], ALU.add).then_inc(s["pa"], 1)
                            else:
                                v.tensor_tensor(blk(a, b, 0, HC), blk(a, b, 0, HC), part_f[:, 0:HC], ALU.add)
                            v.drain()

            for g in (GNN, FFN):
                v.sem_inc(st[g.name]["hist"], 1)
            split_edges(GNN)
            with v.Fori(0, GNN.batches // 2) as i:
                for h in range(2):
                    histogram(GNN, 2 * i + h, h, alone=(h == 0))
            count_groups(GNN)

            v.wait_ge(s_xin, 32)
            with v.Fori(0, NB // 7) as i:
                for j in range(7):
                    mean_var(blk(xn_all, i * 7 + j), i * 7 + j)
            v.drain()
            for b in range(NB):
                v.bn_aggr(mv[:, b, :], stats[:, b, :])
            v.drain().then_inc(s_var, 1)
            v.wait_ge(s_sd, 1)
            v.reciprocal(rstd[:, :], rstd[:, :])
            v.drain()
            normalise(GNN, xn_all, mv)
            ranks(GNN)
            v.wait_ge(s_norm, 16 * 6)
            state(GNN)
            for h in range(2):
                v.wait_ge(st["gnn"]["sc"][h], 16 * BATCH * (GNN.batches // 2))
            split_edges(FFN)

            def next_histogram(b):
                for j in range(HPB):
                    histogram(FFN, b * HPB + j, j % 2, alone=(j == 0))

            attend(GNN, True, next_histogram)
            for j in range(FFN.batches - NB * HPB):
                histogram(FFN, NB * HPB + j, j % 2, alone=(j == 0))
            count_groups(FFN)

            v.drain().then_inc(st["gnn"]["end"], 1)

            v.wait_ge(s_x2, 32)
            with v.Fori(0, NC) as c:
                o = acc[:, bass.ds(c * CH, CH), 0:D]
                dn = acc[:, bass.ds(c * CH, CH), D:GNN.row]
                o4 = o.rearrange("p b (h c) -> p b h c", h=GNN.heads)
                v.tensor_scalar(dn, dn, 1e-16, None, ALU.add)
                v.drain()
                v.reciprocal(dn, dn)
                v.drain()
                v.tensor_tensor(o4, o4, bc(dn.unsqueeze(3), [P, CH, GNN.heads, GNN.width]), ALU.mult)
                v.drain()
                v.tensor_tensor(o, o, bc(par[:, 0:1, :], [P, CH, D]), ALU.add)
                v.drain()
                for j in range(CH):
                    v.bn_stats(stats[:, j, :], blk(acc, c * CH + j, 0, D))
                v.drain()
                for j in range(CH):
                    a_ = v.bn_aggr(mv[:, j, :], stats[:, j, :])
                a_.then_inc(s_sdo, 1)
                v.wait_ge(s_sdo2, c + 1)
                v.reciprocal(rstd[:, 0:CH], rstd[:, 0:CH])
                v.drain()
                for j in range(CH):
                    ob = blk(acc, c * CH + j, 0, D)
                    v.tensor_scalar(ob, ob, mv[:, j, 0:1], rstd[:, j:j + 1], ALU.subtract, ALU.mult)
                v.drain()
                v.tensor_tensor(o, o, bc(par[:, 1:2, :], [P, CH, D]), ALU.mult)
                v.drain()
                v.tensor_tensor(o, o, bc(par[:, 2:3, :], [P, CH, D]), ALU.add)
                v.drain()
                v.tensor_tensor(o, o, xn_all[:, bass.ds(c * CH, CH), :], ALU.add)
                v.drain()
                for j in range(CH):
                    v.bn_stats(stats[:, j, :], blk(acc, c * CH + j, 0, D))
                v.drain()
                for j in range(CH):
                    v.bn_aggr(mv[:, j, :], stats[:, j, :])
                v.drain()
                v.tensor_copy(mv2[:, bass.ds(c * CH, CH), :], mv[:, 0:CH, :])
                v.drain()
            v.drain().then_inc(s_var, 1)
            v.wait_ge(s_sd, 2)
            v.reciprocal(rstd[:, :], rstd[:, :])
            v.drain()

            normalise(FFN, acc, mv2)
            ranks(FFN)
            state(FFN)
            for h in range(2):
                v.wait_ge(st["ffn"]["sc"][h], 16 * BATCH * (FFN.batches // 2))
            v.sem_inc(s_ys, 16)
            v.sem_inc(s_yu, 2)
            v.wait_ge(s_par, 16 * (3 * NE + 1))

            def expert_outputs(b):
                v.wait_ge(s_ys, b * 16 + 16)
                for e in range(NE):
                    v.wait_ge(s_y, b * NE + e + 3)
                    m = v.tensor_tensor(y[:, e, :], bank[2 + e % 2][:, 0:D], b2b[:, e, :], ALU.add)
                    m.then_inc(s_yu, 1)
                v.drain().then_inc(s_yr, 1)

            attend(FFN, False, expert_outputs)

            fo = facc[:, :, 0:16]
            fd = facc[:, :, 16:20]
            v.tensor_scalar(fd, fd, 1e-16, None, ALU.add)
            v.drain()
            v.reciprocal(fd, fd)
            v.drain()
            v.tensor_tensor(fo.rearrange("p b (h c) -> p b h c", h=FHEADS), fo.rearrange("p b (h c) -> p b h c", h=FHEADS),
                            bc(fd.unsqueeze(3), [P, NB, FHEADS, NE]), ALU.mult)
            v.drain()
            v.tensor_tensor(fo, fo, bc(fpar[:, 0:1, :], [P, NB, 16]), ALU.add)
            v.drain()
            v.tensor_reduce(mv2[:, :, 0], fo, AX.X, ALU.add)
            v.drain()
            v.tensor_scalar(mv2[:, :, 0], mv2[:, :, 0], 1.0 / 16, None, ALU.mult)
            v.drain()
            v.tensor_tensor(fo, fo, bc(mv2[:, :, 0:1], [P, NB, 16]), ALU.subtract)
            v.drain()
            v.tensor_tensor(lnf[:, :, :], fo, fo, ALU.mult)
            v.drain()
            v.tensor_reduce(mv2[:, :, 1], lnf[:, :, :], AX.X, ALU.add)
            v.drain()
            v.tensor_scalar(mv2[:, :, 1], mv2[:, :, 1], 1.0 / 16, None, ALU.mult)
            v.drain().then_inc(s_zf, 1)
            v.wait_ge(s_zf2, 1)
            v.reciprocal(rstd[:, :], rstd[:, :])
            v.drain()
            v.tensor_tensor(fo, fo, bc(rstd[:, :].unsqueeze(2), [P, NB, 16]), ALU.mult)
            v.drain()
            v.tensor_tensor(fo, fo, bc(fpar[:, 1:2, :], [P, NB, 16]), ALU.mult)
            v.drain()
            v.tensor_tensor(fo, fo, bc(fpar[:, 2:3, :], [P, NB, 16]), ALU.add)
            v.drain()
            v.tensor_reduce(sc[:, :, :], fo.rearrange("p b (h e) -> p b e h", h=FHEADS), AX.X, ALU.add)
            v.drain()
            v.tensor_scalar(sc[:, :, :], sc[:, :, :], 1.0 / FHEADS, None, ALU.mult)
            v.memset(cnt[:, :, :], 0.0)
            v.drain()
            for e in range(NE):
                for o in range(NE):
                    if o != e:
                        v.tensor_tensor(cmp[:, :], sc[:, :, o], sc[:, :, e], ALU.is_ge if o < e else ALU.is_gt)
                        v.drain()
                        v.tensor_tensor(cnt[:, :, e], cnt[:, :, e], cmp[:, :], ALU.add)
                        v.drain()
            v.tensor_reduce(cmp[:, :], sc[:, :, :], AX.X, ALU.max)
            v.drain()
            v.tensor_tensor(sc[:, :, :], sc[:, :, :], bc(cmp[:, :].unsqueeze(2), [P, NB, NE]), ALU.subtract)
            v.tensor_scalar(cnt[:, :, :], cnt[:, :, :], 1.5, None, ALU.is_lt)
            v.drain().then_inc(s_zf, 1)
            v.wait_ge(s_zf2, 2)
            v.tensor_tensor(gate[:, :, :], gate[:, :, :], cnt[:, :, :], ALU.mult)
            v.drain()
            v.tensor_reduce(cmp[:, :], gate[:, :, :], AX.X, ALU.add)
            v.drain()
            v.reciprocal(cmp[:, :], cmp[:, :])
            v.drain()
            v.tensor_tensor(gate[:, :, :], gate[:, :, :], bc(cmp[:, :].unsqueeze(2), [P, NB, NE]), ALU.mult)
            v.drain().then_inc(s_gate, 1)

            with v.Fori(0, NC) as c:
                for j in range(CH):
                    v.wait_ge(s_yb[j], (c + 1) * 16)
                for e in range(NE):
                    for j in range(CH):
                        o = blk(acc, c * CH + j, 0, D)
                        gt = gate[:, bass.ds(c * CH + j, 1), e]
                        v.scalar_tensor_tensor(out=o, in0=yback[:, j, e, :], scalar=gt, in1=o, op0=ALU.mult, op1=ALU.add)
                    v.drain()
                v.engine_nop().then_inc(s_fin, 1)


_INS = ["x", "src", "dst", "L0_gnn_W", "L0_gnn_att_src", "L0_gnn_att_dst", "L0_gnn_bias", "L0_gnn_ln_gamma",
        "L0_gnn_ln_beta", "L0_ffn_W_gat", "L0_ffn_att_src", "L0_ffn_att_dst", "L0_ffn_b_gat", "L0_ffn_ln_gamma",
        "L0_ffn_ln_beta", "L0_ffn_W1", "L0_ffn_b1", "L0_ffn_W2", "L0_ffn_b2", "L0_ffn_edge_index"]


def kernel(**inputs):
    import concourse.bacc as bacc
    from concourse.bass_utils import run_bass_kernel_spmd

    nc = bacc.Bacc("TRN2", target_bir_lowering=False, num_devices=1)
    arrays, args = {}, []
    for name in _INS:
        a = np.ascontiguousarray(inputs[name])
        arrays[f"in_{name}"] = a
        args.append(nc.dram_tensor(f"in_{name}", a.shape, mybir.dt.from_np(a.dtype), kind="ExternalInput").ap())
    args.append(nc.dram_tensor("out", (N, D), F32, kind="ExternalOutput").ap())
    build(nc, *args)
    r = run_bass_kernel_spmd(nc, [arrays], core_ids=[0])
    return r.results[0]["out"]
```

```python
from contextlib import ExitStack

import numpy as np

import concourse.bass as bass
from concourse import mybir
from concourse.alu_op_type import AluOpType as ALU

ACT = mybir.ActivationFunctionType
AX = mybir.AxisListType
F32 = mybir.dt.float32
BF16 = mybir.dt.bfloat16
I32 = mybir.dt.int32
U32 = mybir.dt.uint32

P = 128
N = 6250
D = 256
NB = -(-N // P)
TAIL = N - (NB - 1) * P
EPS = 1e-5
SLOPE = 0.2
SENT = NB * P
LOW = -1e30
OUTSIDE = 1 << 27

UNIT_LOG = 3
UNIT = 1 << UNIT_LOG
RING_LOG = 2
RING = 4
BLOCK_QUADS = NB // 2
FILL_LOG = 3
FILL = 8
MIN_UNITS = (BLOCK_QUADS + 3) * RING
OHS = 4
BATCH = 4
NE, FF = 4, 512
FT = FF // P
KT = D // P
FHEADS = 4
CH = 7
NC = NB // CH
HPB = 5


class Graph:

    def __init__(self, name, edges, heads, width):
        self.name, self.edges, self.heads, self.width = name, edges, heads, width
        self.hc = heads * width
        self.row = self.hc + 2 * heads
        tiles = -(-edges // P)
        self.tiles = -(-tiles // (OHS * BATCH)) * OHS * BATCH
        self.batches = self.tiles // BATCH
        self.units = (edges // UNIT + NB + MIN_UNITS) // RING * RING
        self.filled = -(-(edges // (P * UNIT) + NB) // FILL)


GNN = Graph("gnn", 100000, 8, 32)
FFN = Graph("ffn", 131072, FHEADS, NE)


def build(nc, x, src, dst, W, att_src, att_dst, bias, gamma, beta, W_gat, fatt_src, fatt_dst, b_gat,
          fgamma, fbeta, W1, b1, W2, b2, edge_index, out):
    ctx = ExitStack()
    with ctx:
        def sb(name, shape, dt=F32):
            return ctx.enter_context(nc.sbuf_tensor(name, shape, dt))

        def sem(name):
            return ctx.enter_context(nc.semaphore(name))

        bank = [ctx.enter_context(nc.psum_tensor(f"bank{i}", [P, 512], F32)) for i in range(8)]

        UK = -(-max(GNN.units, FFN.units) // P)

        table = {g.name: nc.dram_tensor(f"table_{g.name}", [SENT + 1, g.row], F32).ap() for g in (GNN, FFN)}
        y_dram = nc.dram_tensor("y_dram", [NB * P, NE * D], F32).ap()
        ell = {g.name: nc.dram_tensor(f"ell_{g.name}", [(g.units + 2 * FILL) * P * UNIT, 1], U32).ap() for g in (GNN, FFN)}
        unit_block = {g.name: nc.dram_tensor(f"unit_block_{g.name}", [P * UK, 1], I32).ap() for g in (GNN, FFN)}
        out_dram = {g.name: nc.dram_tensor(f"attended_{g.name}", [SENT, g.hc], F32).ap() for g in (GNN, FFN)}

        acc = sb("acc", [P, NB, GNN.row])
        work = sb("work", [P, NB * D])
        xn_all = work[:, :].rearrange("p (b d) -> p b d", b=NB)
        ring_w = UNIT * GNN.row
        ring = {GNN.name: [work[:, s * ring_w:(s + 1) * ring_w].rearrange("p (r w) -> p r w", r=UNIT)
                           for s in range(RING)]}
        prod_w = UNIT * GNN.hc
        prod_gnn = work[:, RING * ring_w:RING * ring_w + prod_w].rearrange("p (r w) -> p r w", r=UNIT)
        xn2T = work[:, :].rearrange("p (k t) -> p k t", k=KT)
        facc = sb("facc", [P, NB, FFN.row])
        accs = {GNN.name: acc, FFN.name: facc}
        mrun = {g.name: sb(f"mrun_{g.name}", [P, NB, g.heads]) for g in (GNN, FFN)}
        tmpm = sb("tmpm", [P, NB, 8])

        TM = FFN.tiles
        edge_buf = sb("edge_buf", [P, 5 * TM], I32)
        dst_i, src_i, t_i, lane_slot = (edge_buf[:, i * TM:(i + 1) * TM] for i in range(4))
        t_f = edge_buf[:, 4 * TM:5 * TM].bitcast(F32)
        hh = edge_buf[:, 0:NE * FT * P].bitcast(F32).rearrange("p (e f t) -> p e f t", e=NE, f=FT)
        y = edge_buf[:, 3 * TM:3 * TM + NE * D].bitcast(F32).rearrange("p (e d) -> p e d", e=NE)
        fring_w = UNIT * FFN.row
        fbuf = edge_buf[:, 2 * TM:2 * TM + RING * fring_w + 2 * UNIT * FFN.hc].bitcast(F32)
        ring[FFN.name] = [fbuf[:, s * fring_w:(s + 1) * fring_w].rearrange("p (r w) -> p r w", r=UNIT) for s in range(RING)]
        fprod = fbuf[:, RING * fring_w:].rearrange("p (s r w) -> p s r w", s=2, r=UNIT)
        hi_b = sb("hi_b", [P, TM], BF16)
        lo_b = sb("lo_b", [P, TM], BF16)
        OL = sb("OL", [P, OHS, BATCH, P], BF16)
        OH = sb("OH", [P, OHS, BATCH, NB], BF16)
        evenh = sb("evenh", [NB, P])
        Tm = sb("Tm", [P, 2, BATCH, P], BF16)
        TW = BATCH * P
        rank_buf = sb("rank_buf", [P, 4 * TW])
        OHT = rank_buf[0:NB, 0:2 * TW].rearrange("p (s k e) -> p s k e", s=2, k=BATCH)
        Hc = rank_buf[0:NB, 2 * TW:3 * TW].rearrange("p (k e) -> p k e", k=BATCH)
        junk = rank_buf[:, 3 * TW:4 * TW].rearrange("p (k e) -> p k e", k=BATCH)
        prod = {GNN.name: [prod_gnn, rank_buf[:, 0:prod_w].rearrange("p (r w) -> p r w", r=UNIT)], FFN.name: [fprod[:, s] for s in range(2)]}
        rank = sb("rank", [P, BATCH])
        rank_i = sb("rank_i", [P, BATCH], I32)
        q_i = sb("q_i", [P, BATCH], I32)
        b_i = sb("b_i", [P, BATCH], I32)
        addr = sb("addr", [P, OHS, BATCH], U32)
        load = sb("load", [P, OHS, BATCH], U32)
        sent_i = sb("sent_i", [P, FILL * UNIT], U32)
        unit_round = sb("unit_round", [P, UK])
        block_of_unit = rank_buf[:, 0:UK].bitcast(I32)
        block_sum = rank_buf[:, UK:2 * UK]
        lane_f = sb("lane_f", [P, 1])
        deg = sb("deg", [P, NB])
        key = sb("key", [P, NB])
        place = sb("place", [P, NB])
        sdeg = sb("sdeg", [P, NB])
        seed = sb("seed", [P, NB])
        order = {g.name: sb(f"order_{g.name}", [P, NB], U32) for g in (GNN, FFN)}
        scratch = {g.name: t.rearrange("p (b c) -> p b c", b=NB)
                   for g, t in ((GNN, acc[:, :, :].rearrange("p b w -> p (b w)")[:, 0:NB * NB]), (FFN, work[:, 0:NB * NB]))}
        unit_begins = {g: t.rearrange("p (u b) -> p u b", u=UK)
                       for g, t in ((GNN.name, acc[:, :, :].rearrange("p b w -> p (b w)")[:, 0:UK * (NB - 1)]), (FFN.name, work[:, 0:UK * (NB - 1)]))}
        ub = sb("ub", [1, RING], I32)
        ub_own = sb("ub_own", [1, RING], I32)
        ng = sb("ng", [NB, 1])
        ngi = sb("ngi", [NB, 1], I32)
        ngr = sb("ngr", [NB, P])
        cum = {g.name: sb(f"cum_{g.name}", [1, NB + 3], I32) for g in (GNN, FFN)}
        idx = sb("idx", [P, RING, UNIT], U32)

        identf = sb("identf", [P, P])
        identb = sb("identb", [P, P], BF16)
        maskb = sb("maskb", [P, P], BF16)
        upper = sb("upper", [NB, NB + 1])
        iota_f = junk[:, 1, :].bitcast(I32)
        lane_i = junk[:, 2, 0:1].bitcast(I32)
        iota_b = sb("iota_b", [P, P], BF16)
        zero_b = sb("zero_b", [P, P], BF16)
        eps_t = sb("eps_t", [P, 1])
        sent_row = sb("sent_row", [1, GNN.row + FFN.row])

        attb = sb("attb", [P, 2, D])
        wx = sb("wx", [P, KT, D + 16])
        fwx = sb("fwx", [P, KT, 16 + 8])
        fattb = sb("fattb", [P, 2, 16])
        par = sb("par", [P, 3, D])
        fpar = sb("fpar", [P, 3, 16])
        w1 = sb("w1", [P, KT, NE, FF])
        w2 = sb("w2", [P, FT, NE, D])
        b1t = sb("b1t", [P, NE, FT])
        b2b = sb("b2b", [P, NE, D])
        yback = work[:, 0:CH * NE * D].rearrange("p (s e d) -> p s e d", s=CH, e=NE)

        stats = sb("stats", [P, NB, 6])
        mv = sb("mv", [P, NB, 2])
        rstd = sb("rstd", [P, NB])
        mv2 = sb("mv2", [P, NB, 2])
        xT = sb("xT", [P, KT, P])
        xnrm = sb("xnrm", [P, D])
        zt = sb("zt", [P, UNIT, 8])
        ed = sb("ed", [P, 2, (UNIT + 1) * 8])
        wt = sb("wt", [P, 2, (UNIT + 1) * 8])
        gm = sb("gm", [P, 8])
        mnew = sb("mnew", [P, 8])
        den_p = sb("den_p", [P, 2, 8])
        part_f = sb("part_f", [P, 16])
        sc = tmpm[:, :, :].rearrange("p b h -> p (b h)")[:, 0:NB * NE].rearrange("p (b e) -> p b e", e=NE)
        cnt = tmpm[:, :, :].rearrange("p b h -> p (b h)")[:, NB * NE:2 * NB * NE].rearrange("p (b e) -> p b e", e=NE)
        cmp = sb("cmp", [P, NB])
        lnf = t_f[:, 0:NB * FFN.hc].rearrange("p (b c) -> p b c", b=NB)
        gate = t_f[:, NB * FFN.hc:NB * (FFN.hc + NE)].rearrange("p (b e) -> p b e", e=NE)

        s_par = sem("s_par")
        s_att = sem("s_att")
        s_norm = sem("s_norm")
        s_xin = sem("s_xin")
        s_xpad = sem("s_xpad")
        s_const = sem("s_const")
        s_cv = sem("s_cv")
        s_wx = sem("s_wx")
        s_var = sem("s_var")
        s_sd = sem("s_sd")
        st = {}
        for g in (GNN, FFN):
            n = g.name
            st[n] = dict(
                xn=sem(f"{n}_xn_ready"),
                tp=sem(f"{n}_xT_in_psum"),
                tc=sem(f"{n}_xT_copied"),
                pj=sem(f"{n}_proj_done"),
                pc=sem(f"{n}_proj_copied"),
                tab=sem(f"{n}_table_written"),
                raw=sem(f"{n}_edges_landed"),
                fill=sem(f"{n}_edge_pad_written"),
                prep=sem(f"{n}_edges_split"),
                oh=sem(f"{n}_onehots_ready"),
                hist=sem(f"{n}_histogram_batch_done"),
                seeded=sem(f"{n}_histogram_seeded"),
                cumr=sem(f"{n}_unit_sums_in_psum"),
                cumw=sem(f"{n}_unit_sums_ready"),
                pre=sem(f"{n}_ell_prefilled"),
                oh2=sem(f"{n}_rank_onehots_ready"),
                fr=sem(f"{n}_front_in_psum"),
                oht=sem(f"{n}_onehot_T_copied"),
                tm=sem(f"{n}_pairs_ready"),
                hu=sem(f"{n}_running_histogram_updated"),
                hcp=sem(f"{n}_running_histogram_copied"),
                gr=sem(f"{n}_lookup_ready"),
                ranked=sem(f"{n}_ranks_read"),
                ad=sem(f"{n}_slots_ready"),
                seedin=sem(f"{n}_seed_inputs_ready"),
                sc=[sem(f"{n}_scattered{s}") for s in range(OHS)],
                ix=[sem(f"{n}_index_landed{s}") for s in range(RING)],
                ga=[sem(f"{n}_rows_landed{s}") for s in range(RING)],
                ru=sem(f"{n}_rows_used"),
                noted=sem(f"{n}_unit_noted"),
                ed=sem(f"{n}_logits_ready"),
                w=sem(f"{n}_weights_ready"),
                pr=sem(f"{n}_products_ready"),
                ps=sem(f"{n}_products_summed"),
                pa=sem(f"{n}_sums_added"),
                end=sem(f"{n}_attended"),
                ct=sem(f"{n}_ordering_input_ready"),
                cp=sem(f"{n}_ordering_product_in_psum"),
                sg=sem(f"{n}_ordered_rows_landed"),
                fin=sem(f"{n}_blocks_attended_finished"),
                back=sem(f"{n}_results_in_node_order"),
                rs=sem(f"{n}_results_scattered"),
            )
        s_x2 = sem("s_x_landed_again")
        s_sdo = sem("s_out_var_ready")
        s_sdo2 = sem("s_out_sd_ready")
        s_zf = sem("s_gate_exp_in")
        s_zf2 = sem("s_gate_exp_out")
        s_gate = sem("s_gate_ready")
        s_h1 = sem("s_hidden_in_psum")
        s_h1u = sem("s_hidden_activated")
        s_y = sem("s_expert_out_in_psum")
        s_yu = sem("s_expert_out_added")
        s_yr = sem("s_expert_outputs_ready")
        s_ys = sem("s_expert_outputs_stored")
        s_yb = [sem(f"s_expert_outputs_back{i}") for i in range(CH)]
        s_yfree = sem("s_expert_outputs_used")
        s_fin = sem("s_chunk_final")
        s_out = sem("s_out_stored")
        s_vstep = sem("s_dve_step")
        s_step = sem("s_pool_step")

        block = ctx.enter_context(nc.Block())

        def bc(ap, shape):
            return ap.to_broadcast(shape)

        hidden_bank = (0, 1, 6, 7)

        def rank_steps(g, engine, step):
            last = g.batches // OHS - 1
            for j in range(OHS):
                step(0, j, True)
            with engine.Fori(1, min(NB, last)) as i:
                for j in range(OHS):
                    step(i, j, True)
            if last > NB:
                with engine.Fori(NB, last) as i:
                    for j in range(OHS):
                        step(i, j, False)
            for j in range(OHS):
                step(last, j, last < NB)

        def quads_of(g, engine, body, per_block=None, lag=0):
            def quad(q, last=False):
                for half in range(2):
                    body(q, half, last)
                    if per_block and not (isinstance(q, int) and not 0 <= 2 * q + half - lag < NB):
                        per_block(2 * q + half - lag)

            quad(0)
            with engine.Fori(1, BLOCK_QUADS) as q:
                quad(q)
            quad(BLOCK_QUADS)
            last = engine.value_load(cum[g.name][0:1, NB + 1:NB + 2], min_val=MIN_UNITS // RING - 1, max_val=g.units // RING - 1)
            per_block = None
            with engine.Fori(BLOCK_QUADS + 1, last) as q:
                quad(q)
            quad(last, last=True)
            return last

        @block.sync
        def _(sp):
            sp.sem_inc(s_fin, 1)
            sp.sem_inc(s_yfree, CH)
            sp.wait_ge(s_xpad, 1)
            sp.dma_start(xn_all[:, 0:NB - 1, :], x[0:(NB - 1) * P, :].rearrange("(b p) d -> p b d", p=P)).then_inc(s_xin, 16)
            sp.dma_start(xn_all[0:TAIL, NB - 1, :], x[(NB - 1) * P:N, :]).then_inc(s_xin, 16)
            sp.dma_start(wx[:, :, 0:D], W.rearrange("(k p) n -> p k n", p=P)).then_inc(s_att, 16)
            sp.dma_start(attb[:, 0, :], att_src.rearrange("(a h) c -> a (h c)", a=1).to_broadcast([P, D])).then_inc(s_att, 16)
            sp.dma_start(attb[:, 1, :], att_dst.rearrange("(a h) c -> a (h c)", a=1).to_broadcast([P, D])).then_inc(s_att, 16)
            sp.dma_start(fwx[:, :, 0:16], W_gat.rearrange("(k p) n -> p k n", p=P)).then_inc(s_att, 16)
            sp.dma_start(fattb[:, 0, :], fatt_src.rearrange("(a h) c -> a (h c)", a=1).to_broadcast([P, 16])).then_inc(s_att, 16)
            sp.dma_start(fattb[:, 1, :], fatt_dst.rearrange("(a h) c -> a (h c)", a=1).to_broadcast([P, 16])).then_inc(s_att, 16)
            raw = st["gnn"]["raw"]
            T = GNN.tiles
            full = GNN.edges // T
            rest = GNN.edges - full * T
            sp.wait_ge(st["gnn"]["fill"], 1)
            for to, of in ((dst_i, dst), (src_i, src)):
                sp.dma_start(to[0:full, 0:T], of[0:full * T].rearrange("(p t) -> p t", t=T)).then_inc(raw, 16)
                sp.dma_start(to[full:full + 1, 0:rest], of[full * T:GNN.edges].rearrange("(p t) -> p t", p=1)).then_inc(raw, 16)
            for i, v in enumerate((bias, gamma, beta)):
                sp.dma_start(par[:, i, :], v.rearrange("(a d) -> a d", a=1).to_broadcast([P, D])).then_inc(s_norm, 16)
            for i, v in enumerate((b_gat, fgamma, fbeta)):
                sp.dma_start(fpar[:, i, :], v.rearrange("(a d) -> a d", a=1).to_broadcast([P, 16])).then_inc(s_norm, 16)
            for e in range(NE):
                sp.dma_start(w1[:, :, e, :], W1[e].rearrange("(k p) f -> p k f", p=P)).then_inc(s_par, 16)
                sp.dma_start(w2[:, :, e, :], W2[e].rearrange("(f p) d -> p f d", p=P)).then_inc(s_par, 16)
                sp.dma_start(b2b[:, e, :], b2[e:e + 1, :].to_broadcast([P, D])).then_inc(s_par, 16)
            with nc.allow_non_contiguous_dma(reason="b1 by hidden unit on the partitions"):
                sp.dma_start(b1t[:, :, :], b1.rearrange("e (f p) -> p e f", p=P)).then_inc(s_par, 16)

            def tables(g, off):
                s = st[g.name]
                for c in range(NC):
                    sp.wait_ge(s["pc"], (c + 1) * CH)
                    sp.dma_start(table[g.name][c * CH * P:(c + 1) * CH * P, :].rearrange("(b p) w -> p b w", p=P),
                                 accs[g.name][:, c * CH:(c + 1) * CH, :]).then_inc(s["tab"], 16)
                sp.dma_start(table[g.name][SENT:SENT + 1, :], sent_row[:, off:off + g.row]).then_inc(s["tab"], 16)

            def fill(g, i):
                sp.dma_start(ell[g.name][bass.ds(i * (FILL * P * UNIT), FILL * P * UNIT), :].rearrange("(p r) o -> p (r o)", p=P),
                             sent_i[:, :]).then_inc(st[g.name]["pre"], 16)

            def prefill(g):
                s = st[g.name]
                sp.wait_ge(s["cumw"], 1)
                sp.dma_start(unit_block[g.name].rearrange("(p k) o -> p (k o)", p=P), block_of_unit).then_inc(s["pre"], 16)
                more = sp.value_load(cum[g.name][0:1, NB + 2:NB + 3], min_val=1, max_val=g.units // FILL - g.filled + 2)
                with sp.Fori(0, more) as i:
                    fill(g, i + g.filled)
                sp.wait_ge(s["pre"], more * 16 + 16 * (g.filled + 1))
                sp.sem_inc(s["cumw"], 1)

            def indices(g, store=None):
                s = st[g.name]
                for h in range(OHS):
                    sp.wait_ge(s["sc"][h], 16 * BATCH * (g.batches // OHS))

                def load(q, half, last=False):
                    for h in (2 * half, 2 * half + 1):
                        u = RING * q + h
                        sp.wait_ge(s["noted"], u + 1)
                        sp.dma_start(idx[:, h, :], ell[g.name][bass.ds(u * (P * UNIT), P * UNIT), :].rearrange("(p r) o -> p (r o)", p=P)).then_inc(s["ix"][h], 16)
                        sp.dma_start(ub[:, h:h + 1], unit_block[g.name][bass.ds(u, 1), :]).then_inc(s["ix"][h], 16)

                sp.sem_inc(s["noted"], RING)
                quads_of(g, sp, load, store, lag=2)
                if store:
                    store(NB - 1)

            def store_y(b):
                sp.wait_ge(s_yr, b + 1)
                sp.dma_start(y_dram[bass.ds(b * P, P), :], y.rearrange("p e d -> p (e d)")).then_inc(s_ys, 16)

            def back(g):
                s = st[g.name]
                sp.wait_ge(s["rs"], 16 * NB)
                sp.dma_start(accs[g.name][:, :, 0:g.hc], out_dram[g.name].rearrange("(b p) w -> p b w", p=P)).then_inc(s["back"], 16)

            sp.wait_ge(s_const, 1)
            for g in (GNN, FFN):
                for i in range(g.filled):
                    fill(g, i)
            prefill(GNN)
            tables(GNN, 0)
            for h in range(OHS):
                sp.wait_ge(st["gnn"]["sc"][h], 16 * BATCH * (GNN.batches // OHS))
            T = FFN.tiles
            sp.dma_start(dst_i, edge_index[1].rearrange("(p t) -> p t", t=T)).then_inc(st["ffn"]["raw"], 16)
            sp.dma_start(src_i, edge_index[0].rearrange("(p t) -> p t", t=T)).then_inc(st["ffn"]["raw"], 16)
            indices(GNN)
            sp.wait_ge(st["gnn"]["end"], 1)
            sp.dma_start(xn_all[:, 0:NB - 1, :], x[0:(NB - 1) * P, :].rearrange("(b p) d -> p b d", p=P)).then_inc(s_x2, 16)
            sp.dma_start(xn_all[0:TAIL, NB - 1, :], x[(NB - 1) * P:N, :]).then_inc(s_x2, 16)
            prefill(FFN)
            back(GNN)
            tables(FFN, GNN.row)
            indices(FFN, store_y)

            def y_back(c):
                for j in range(CH):
                    sp.wait_ge(s_yfree, c * CH + j + 1)
                    sp.dma_start(yback[:, j].rearrange("p e d -> p (e d)"), y_dram[bass.ds((c * CH + j) * P, P), :]).then_inc(s_yb[j], 16)

            sp.wait_ge(s_ys, 16 * NB + 16)
            y_back(0)
            back(FFN)
            with sp.Fori(1, NC) as c:
                y_back(c)
            sp.wait_ge(s_out, 16 * (NC + 1))

        @block.gpsimd
        def _(pool):
            pool.memset(identf[:, :], 0.0)
            pool.memset(upper[:, :], 1.0)
            pool.memset(sent_row[:, :], 0.0)
            pool.drain()
            pool.memset(sent_row[0:1, GNN.hc:GNN.hc + GNN.heads], LOW)
            pool.memset(sent_row[0:1, GNN.row + FFN.hc:GNN.row + FFN.hc + FFN.heads], LOW)
            pool.iota(iota_f[:, :], pattern=[[1, P]], base=0, channel_multiplier=0)
            pool.iota(sent_i[:, :], pattern=[[0, FILL * UNIT]], base=SENT, channel_multiplier=0)
            pool.iota(block_of_unit, pattern=[[UNIT, UK]], base=0, channel_multiplier=UNIT * UK)
            pool.iota(lane_i, pattern=[[0, 1]], base=0, channel_multiplier=1)
            pool.affine_select(out=identf[:, :], in_=identf[:, :], compare_op=ALU.not_equal, fill=1.0,
                               base=0, pattern=[[-1, P]], channel_multiplier=1)
            pool.affine_select(out=upper[:, :], in_=upper[:, :], compare_op=ALU.is_gt, fill=0.0,
                               base=0, pattern=[[1, NB + 1]], channel_multiplier=-1)
            pool.memset(junk[:, 0, :], float(1 << 20))
            pool.drain()
            pool.affine_select(out=junk[:, 0, :], in_=junk[:, 0, :], compare_op=ALU.is_ge, fill=0.0,
                               base=0, pattern=[[-1, P]], channel_multiplier=1)
            pool.drain().then_inc(s_const, 1)

            def scatters(g):
                s = st[g.name]
                pool.wait_ge(s["cumw"], 2)
                with pool.Fori(0, g.batches // OHS) as i:
                    for h in range(OHS):
                        pool.wait_ge(s["ad"], OHS * i + h + 1)
                        pool.sem_inc(s_step, 1)
                        for k in range(BATCH):
                            pool.indirect_dma_start(ell[g.name], bass.IndirectOffsetOnAxis(addr[:, h, k:k + 1], 0),
                                                    load[:, h, k:k + 1], None, bounds_check=g.units * P * UNIT - 1,
                                                    oob_is_err=False).then_inc(s["sc"][h], 16)

            def ordered_rows(g):
                s = st[g.name]
                pool.wait_ge(s["tab"], 16 * (NC + 1))
                pool.wait_ge(s["seedin"], 1)
                pool.sem_inc(s_step, 1)
                for b in range(NB):
                    pool.indirect_dma_start(accs[g.name][:, b, :], None, table[g.name],
                                            bass.IndirectOffsetOnAxis(order[g.name][:, b:b + 1], 0)).then_inc(s["sg"], 16)

            def gathers(g):
                s = st[g.name]
                pool.sem_inc(s["ru"], RING)

                def gather(q, half, last):
                    for h in (2 * half, 2 * half + 1):
                        pool.wait_ge(s["ix"][h], (q + 1) * 32)
                        pool.wait_ge(s["ru"], RING * q + h + 1)
                        pool.sem_inc(s_step, 1)
                        for r in range(UNIT):
                            pool.indirect_dma_start(ring[g.name][h][:, r, :], None, table[g.name],
                                                    bass.IndirectOffsetOnAxis(idx[:, h, r:r + 1], 0)).then_inc(s["ga"][h], 16)

                quads_of(g, pool, gather)

            def results(g):
                s = st[g.name]
                for c in range(NC):
                    pool.wait_ge(s["fin"], c + 1)
                    pool.sem_inc(s_step, 1)
                    for b in range(c * CH, (c + 1) * CH):
                        pool.indirect_dma_start(out_dram[g.name], bass.IndirectOffsetOnAxis(order[g.name][:, b:b + 1], 0),
                                                accs[g.name][:, b, 0:g.hc], None).then_inc(s["rs"], 16)

            for g in (GNN, FFN):
                scatters(g)
                ordered_rows(g)
                gathers(g)
                results(g)


        @block.scalar
        def _(act):
            def deviations(stage):
                act.wait_ge(s_var, stage)
                act.activation(rstd[:, :], (mv if stage == 1 else mv2)[:, :, 1], ACT.Sqrt, bias=eps_t[:, 0:1]).then_inc(s_sd, 1)

            def transposed(g, b):
                s = st[g.name]
                act.wait_ge(s["tp"], b + 1)
                if not isinstance(b, int) or b > 0:
                    act.wait_ge(s["pj"], b)
                rows_t = bank[7][:, 0:D].rearrange("p (k t) -> p k t", k=KT)
                if g is FFN:
                    act.activation(xn2T[:, :, bass.ds(b * P, P)], rows_t, ACT.Copy)
                act.activation(xT[:, :, :], rows_t, ACT.Copy).then_inc(s["tc"], 1)

            def ranks(g):
                s = st[g.name]
                act.wait_ge(s["seeded"], 1)
                act.wait_ge(s["cumw"], 2)
                for c in range(2):
                    act.activation(Hc[:, c, :], bank[c][0:NB, 0:P], ACT.Copy).then_inc(s["hcp"], 1)

                def onehot(n, h):
                    act.wait_ge(s["fr"], n + 1)
                    act.activation(OHT[:, h], bank[6][0:NB, 0:BATCH * P // 2].bitcast(BF16).rearrange("p (k e) -> p k e", k=BATCH), ACT.Copy).then_inc(s["oht"], 1)

                def step(i, j, project):
                    n = OHS * i + j
                    if not isinstance(n, int) or n < g.batches - 1:
                        onehot(n + 1, (j + 1) % 2)
                    if project and j == 2:
                        transposed(g, i)
                    for k in range(BATCH):
                        act.wait_ge(s["hu"], n * BATCH + k + 1)
                        act.activation(Hc[:, (k + 2) % BATCH, :], bank[k % 2][0:NB, 0:P], ACT.Copy).then_inc(s["hcp"], 1)

                onehot(0, 0)
                rank_steps(g, act, step)

            def weights(g, per_block=None):
                s = st[g.name]
                w = (UNIT + 1) * g.heads

                def exps(q, half, last):
                    for h in range(2):
                        act.wait_ge(s["ed"], RING * q + 2 * half + h + 1)
                        act.activation(wt[:, h, 0:w], ed[:, h, 0:w], ACT.Exp).then_inc(s["w"], 1)

                quads_of(g, act, exps, per_block)

            def hidden(b):
                for e in range(NE):
                    act.wait_ge(s_h1, b * NE + e + 1)
                    act.wait_ge(s_y, b * NE + e + 1)
                    for f in range(FT):
                        m = act.activation(hh[:, e, f, :], bank[hidden_bank[e]][:, f * P:(f + 1) * P], ACT.Gelu, bias=b1t[:, e, f:f + 1])
                    m.then_inc(s_h1u, 1)

            act.wait_ge(s_cv, 1)
            deviations(1)
            ranks(GNN)
            weights(GNN)
            with act.Fori(0, NC) as c:
                act.wait_ge(s_sdo, c + 1)
                act.activation(rstd[:, 0:CH], mv[:, 0:CH, 1], ACT.Sqrt, bias=eps_t[:, 0:1]).then_inc(s_sdo2, 1)
            deviations(2)
            ranks(FFN)
            act.wait_ge(s_par, 16 * (3 * NE + 1))
            act.sem_inc(s_h1u, NE)
            act.sem_inc(s_y, NE)
            for h in range(OHS):
                act.wait_ge(st["ffn"]["sc"][h], 16 * BATCH * (FFN.batches // OHS))
            weights(FFN, hidden)
            act.wait_ge(s_zf, 1)
            act.activation(rstd[:, :], mv2[:, :, 1], ACT.Sqrt, bias=eps_t[:, 0:1]).then_inc(s_zf2, 1)
            act.wait_ge(s_zf, 2)
            act.activation(gate[:, :, :], sc, ACT.Exp).then_inc(s_zf2, 1)
            with act.Fori(0, NC - 1) as c:
                act.wait_ge(s_fin, c + 2)
                act.dma_start(out[bass.ds(c * (CH * P), CH * P), :].rearrange("(b p) d -> p b d", p=P), acc[:, bass.ds(c * CH, CH), 0:D]).then_inc(s_out, 16)
            act.wait_ge(s_fin, NC + 1)
            act.dma_start(out[(NC - 1) * CH * P:(NB - 1) * P, :].rearrange("(b p) d -> p b d", p=P), acc[:, (NC - 1) * CH:NB - 1, 0:D]).then_inc(s_out, 16)
            act.dma_start(out[(NB - 1) * P:N, :], acc[0:TAIL, NB - 1, 0:D]).then_inc(s_out, 16)

        @block.tensor
        def _(pe):
            def transpose_rows(g, b):
                s = st[g.name]
                pe.wait_ge(s["xn"], b + 1)
                if not isinstance(b, int) or b > 0:
                    pe.wait_ge(s["pc"], b)
                for k in range(KT):
                    t = pe.transpose(bank[7][:, k * P:(k + 1) * P], xnrm[:, k * P:(k + 1) * P], identf[:, :])
                t.then_inc(s["tp"], 1)

            def project_rows(g, b):
                s = st[g.name]
                wgt = wx if g is GNN else fwx
                pe.wait_ge(s["tc"], b + 1)
                for k in range(KT):
                    m = pe.matmul(bank[7][:, 0:g.row], xT[:, k, :], wgt[:, k, 0:g.row], start=(k == 0), stop=(k == KT - 1))
                m.then_inc(s["pj"], 1)

            def start_histogram():
                for c in range(2):
                    pe.matmul(bank[c][0:NB, 0:P], zero_b[:, 0:NB], zero_b[:, :], start=True, stop=False, skip_group_check=True)

            def histogram(g, n, h):
                s = st[g.name]
                pe.wait_ge(s["oh"], n + 1)
                for k in range(BATCH):
                    m = pe.matmul(bank[k % 2][0:NB, 0:P], OH[:, h, k, :], OL[:, h, k, :], start=False, stop=False, skip_group_check=True)
                m.then_inc(s["hist"], 1)

            def end_histogram(g):
                s = st[g.name]
                pe.wait_ge(s["ct"], 1)
                pe.matmul(bank[2][0:P, 0:NB], ngr[:, :], identf[0:NB, 0:NB], start=True, stop=True).then_inc(s["cp"], 1)
                pe.wait_ge(s["ct"], 2)
                pe.matmul(bank[3][0:NB, 0:P], sdeg[:, :], identf[:, :], start=True, stop=True).then_inc(s["cp"], 1)
                pe.wait_ge(s["ct"], 3)
                pe.matmul(bank[2][0:1, 0:NB + 1], ng[:, 0:1], upper[:, :], start=True, stop=True)
                pe.matmul(bank[3][0:P, 0:NB], ngr[:, :], upper[:, 0:NB], start=True, stop=True).then_inc(s["cp"], 1)

            def ranks(g):
                s = st[g.name]
                pe.wait_ge(s["seedin"], 1)
                pe.matmul(bank[0][0:NB, 0:P], seed[:, :], identf[:, :], start=True, stop=False, skip_group_check=True)
                pe.matmul(bank[1][0:NB, 0:P], seed[:, :], identf[:, :], start=True, stop=False, skip_group_check=True)
                pe.matmul(bank[1][0:NB, 0:P], identf[0:NB, 0:NB], evenh[:, :], start=False, stop=False, skip_group_check=True).then_inc(s["seeded"], 1)

                def front(n, o, h):
                    pe.wait_ge(s["oh2"], n + 1)
                    if not isinstance(n, int) or n >= 2:
                        pe.wait_ge(s["tm"], n)
                    pe.matmul(bank[4 + h][:, :], identb[:, :], bc(maskb[:, :].unsqueeze(1), [P, BATCH, P]), start=True, stop=False, skip_group_check=True)
                    for k in range(BATCH):
                        if k == BATCH - 1:
                            pe.wait_ge(s["oht"], n + 1)
                        pe.matmul(bank[4 + h][:, k * P:(k + 1) * P], bc(hi_b[:, bass.ds(n * BATCH + k, 1)], [P, P]), identb[:, :],
                                  start=False, stop=True, skip_group_check=True)
                    for k in range(BATCH):
                        t = pe.transpose(bank[6][0:NB, k * P // 2:(k + 1) * P // 2].bitcast(BF16), OH[:, o, k, :], identb[:, :])
                    t.then_inc(s["fr"], 1)

                def chain(n, o, h):
                    pe.wait_ge(s["oht"], n + 2)
                    pe.wait_ge(s["tm"], n + 2)
                    pe.wait_ge(s["ranked"], n + 1)
                    for k in range(BATCH):
                        col = slice(k * P, (k + 1) * P)
                        pe.matmul(bank[2 + h][:, col], Tm[:, h, k, :], OL[:, o, k, :], start=True, stop=False, skip_group_check=True)
                        pe.wait_ge(s["hcp"], n * BATCH + k + 1)
                        m = pe.matmul(bank[2 + h][:, col], OHT[:, h, k, :], Hc[:, k, :], start=False, stop=True, skip_group_check=True)
                        if k == BATCH - 1:
                            m.then_inc(s["gr"], 1)
                        pe.matmul(bank[k % 2][0:NB, 0:P], OH[:, o, k, :], OL[:, o, k, :], start=False, stop=False, skip_group_check=True).then_inc(s["hu"], 1)

                pe.sem_inc(s["tm"], 1)
                pe.sem_inc(s["oht"], 1)
                front(0, 0, 0)

                def step(i, j, project):
                    n = OHS * i + j
                    if project and j == 1:
                        transpose_rows(g, i)
                    if project and j == 3:
                        project_rows(g, i)
                    if not isinstance(n, int) or n < g.batches - 1:
                        front(n + 1, (j + 1) % OHS, (j + 1) % 2)
                    chain(n, j, j % 2)

                rank_steps(g, pe, step)

            def sums(g, per_block):
                s = st[g.name]

                def add_up(q, half, last):
                    for h in range(2):
                        u = RING * q + 2 * half + h
                        pe.wait_ge(s["pr"], u + 1)
                        pe.wait_ge(s["pa"], u + 1)
                        for r in range(UNIT):
                            m = pe.matmul(bank[4 + h][:, 0:g.hc], identf[:, :], prod[g.name][h][:, r, :], start=(r == 0), stop=(r == UNIT - 1))
                        m.then_inc(s["ps"], 1)

                quads_of(g, pe, add_up, per_block)

            def first(b, e):
                pe.wait_ge(s_h1u, b * NE + e + 1)
                for f in range(FT):
                    for k in range(KT):
                        m = pe.matmul(bank[hidden_bank[e]][:, f * P:(f + 1) * P], w1[:, k, e, f * P:(f + 1) * P], xn2T[:, k, bass.ds(b * P, P)],
                                      start=(k == 0), stop=(k == KT - 1), skip_group_check=True)
                m.then_inc(s_h1, 1)

            def second(b, e):
                pe.wait_ge(s_h1u, b * NE + e + NE + 1)
                pe.wait_ge(s_yu, b * NE + e + 1)
                for f in range(FT):
                    m = pe.matmul(bank[2 + e][:, 0:D], hh[:, e, f, :], w2[:, f, e, :], start=(f == 0), stop=(f == FT - 1))
                m.then_inc(s_y, 1)

            pe.wait_ge(s_const, 1)
            pe.wait_ge(s_cv, 2)
            start_histogram()
            with pe.Fori(0, GNN.batches // OHS) as i:
                for j in range(OHS):
                    histogram(GNN, OHS * i + j, j)
            end_histogram(GNN)
            pe.wait_ge(st["gnn"]["seedin"], 1)
            pe.wait_ge(s_wx, 1)
            ranks(GNN)
            pe.wait_ge(st["gnn"]["hcp"], GNN.tiles + 2)
            start_histogram()

            def next_histogram(b):
                for j in range(HPB):
                    histogram(FFN, b * HPB + j, j % OHS)

            sums(GNN, next_histogram)
            for j in range(FFN.batches - NB * HPB):
                histogram(FFN, NB * HPB + j, j % OHS)
            end_histogram(FFN)
            pe.wait_ge(st["ffn"]["seedin"], 1)
            ranks(FFN)
            pe.wait_ge(st["ffn"]["hcp"], FFN.tiles + 2)
            pe.wait_ge(st["ffn"]["ranked"], FFN.batches + 2)
            pe.wait_ge(st["ffn"]["pc"], NB)
            pe.wait_ge(s_par, 16 * (3 * NE + 1))
            for e in range(NE):
                first(0, e)
            with pe.Fori(0, NB - 1) as b:
                for e in range(NE):
                    second(b, e)
                    first(b + 1, e)
            for e in range(NE):
                second(NB - 1, e)

        @block.vector
        def _(v):
            v.memset(xn_all[:, NB - 1, :], 0.0)
            v.drain().then_inc(s_xpad, 1)
            v.memset(dst_i[:, :], -1)
            v.memset(src_i[:, :], 0)
            v.drain().then_inc(st["gnn"]["fill"], 1)
            v.memset(eps_t[:, :], EPS)
            v.memset(zero_b[:, :], 0.0)
            v.drain().then_inc(s_cv, 1)
            v.wait_ge(s_const, 1)
            v.tensor_copy(iota_b[:, :], iota_f[:, :])
            v.tensor_copy(lane_f[:, :], lane_i)
            v.tensor_copy(unit_round[:, :], block_of_unit)
            v.tensor_copy(identb[:, :], identf[:, :])
            v.tensor_copy(maskb[:, :], junk[:, 0, :])
            v.drain().then_inc(s_cv, 1)
            v.wait_ge(s_att, 16 * 6)
            tmpw = t_f[:, 0:D]
            for (wgt, at, g) in ((wx, attb, GNN), (fwx, fattb, FFN)):
                for k in range(KT):
                    for a in range(2):
                        v.tensor_tensor(tmpw[:, 0:g.hc], wgt[:, k, 0:g.hc], at[:, a, :], ALU.mult)
                        v.drain()
                        v.tensor_reduce(wgt[:, k, g.hc + a * g.heads:g.hc + (a + 1) * g.heads],
                                        tmpw[:, 0:g.hc].rearrange("p (h c) -> p h c", c=g.width), AX.X, ALU.add)
                        v.drain()
            v.drain().then_inc(s_wx, 1)

            def mean_var(of, b):
                v.bn_stats(stats[:, bass.ds(b, 1), :].rearrange("p a s -> p (a s)"), of)

            def blk(t, b, lo=0, hi=None):
                return t[:, bass.ds(b, 1), lo:hi if hi is not None else t.shape[2]].rearrange("p a d -> p (a d)")

            def state(g):
                s = st[g.name]
                a = accs[g.name]
                v.wait_ge(s["sg"], 16 * NB)
                tm = tmpm[:, :, 0:g.heads]
                v.tensor_tensor(tm, a[:, :, g.hc:g.hc + g.heads], a[:, :, g.hc + g.heads:g.row], ALU.add)
                v.drain()
                v.scalar_tensor_tensor(out=mrun[g.name][:, :, :], in0=tm, scalar=SLOPE, in1=tm, op0=ALU.mult, op1=ALU.max)
                v.memset(a[:, :, g.hc:g.hc + g.heads], 1.0)
                v.drain()

            def normalise(g, b):
                s = st[g.name]
                if not isinstance(b, int) or b > 0:
                    v.wait_ge(s["tp"], b)
                of, mean = (xn_all, mv) if g is GNN else (acc, mv2)
                v.tensor_scalar(xnrm[:, :], blk(of, b, 0, D), blk(mean, b, 0, 1), rstd[:, bass.ds(b, 1)], ALU.subtract, ALU.mult).then_inc(s["xn"], 1)

            def projected(g, b):
                s = st[g.name]
                v.wait_ge(s["pj"], b + 1)
                v.tensor_copy(blk(accs[g.name], b), bank[7][:, 0:g.row])
                v.drain().then_inc(s["pc"], 1)

            def split_edges(g):
                s = st[g.name]
                T = g.tiles
                v.wait_ge(s["raw"], 64 if g is GNN else 32)
                di, si, ti, tf = dst_i[:, 0:T], src_i[:, 0:T], t_i[:, 0:T], t_f[:, 0:T]
                v.tensor_scalar(ti, di, 7, None, ALU.logical_shift_right)
                v.tensor_scalar(di, di, P - 1, None, ALU.bitwise_and)
                v.tensor_scalar(tf, si, 0.0, float(N), ALU.is_lt, ALU.mult)
                v.drain()
                v.tensor_copy(hi_b[:, 0:T], ti)
                v.tensor_copy(lo_b[:, 0:T], di)
                v.tensor_tensor(tf, si, tf, ALU.add)
                v.tensor_scalar(lane_slot[:, 0:T], ti, float(NB), float(OUTSIDE), ALU.is_ge, ALU.mult)
                v.drain()
                v.tensor_scalar(si, tf, 0.0, float(N - 1), ALU.max, ALU.min)
                v.tensor_scalar(ti, di, UNIT_LOG, None, ALU.logical_shift_left)
                v.drain()
                v.tensor_tensor(lane_slot[:, 0:T], lane_slot[:, 0:T], ti, ALU.bitwise_or)
                v.drain()

            def onehots(n, o):
                v.tensor_tensor(OL[:, o], bc(iota_b[:, 0:P].unsqueeze(1), [P, BATCH, P]),
                                bc(lo_b[:, bass.ds(n * BATCH, BATCH)].unsqueeze(2), [P, BATCH, P]), ALU.is_equal)
                return v.tensor_tensor(OH[:, o], bc(iota_b[:, 0:NB].unsqueeze(1), [P, BATCH, NB]),
                                       bc(hi_b[:, bass.ds(n * BATCH, BATCH)].unsqueeze(2), [P, BATCH, NB]), ALU.is_equal)

            def histogram(g, n, j):
                if j == 0:
                    v.wait_ge(st[g.name]["hist"], n + 1)
                elif j >= OHS:
                    v.wait_ge(st[g.name]["hist"], n - OHS + 2)
                onehots(n, j % OHS).then_inc(st[g.name]["oh"], 1)

            def order_nodes(g):
                s = st[g.name]
                sq = scratch[g.name]
                row = [P, NB, NB]

                def inner(t):
                    return bc(t[:, 0:NB].unsqueeze(1), row)

                def outer(t):
                    return bc(t[:, 0:NB].unsqueeze(2), row)

                def pick(out, match_outer, match_inner, value):
                    v.tensor_tensor(sq, outer(match_outer), inner(match_inner), ALU.is_equal)
                    v.drain()
                    v.tensor_tensor(sq, sq, inner(value), ALU.mult)
                    v.drain()
                    v.tensor_reduce(out[:, :], sq, AX.X, ALU.add)
                    v.drain()

                v.wait_ge(s["hist"], g.batches + 1)
                v.tensor_copy(evenh[:, :], bank[0][0:NB, 0:P])
                v.drain()
                v.tensor_tensor(ngr[:, :], evenh[:, :], bank[1][0:NB, 0:P], ALU.add).then_inc(s["ct"], 1)
                v.wait_ge(s["cp"], 1)
                v.tensor_copy(deg[:, :], bank[2][:, 0:NB])
                v.drain()
                v.scalar_tensor_tensor(out=key[:, :], in0=deg[:, :], scalar=64.0, in1=iota_b[:, 0:NB], op0=ALU.mult, op1=ALU.subtract)
                v.drain()
                v.tensor_tensor(sq, inner(key), outer(key), ALU.is_gt)
                v.drain()
                v.tensor_reduce(place[:, :], sq, AX.X, ALU.add)
                v.drain()
                pick(sdeg, iota_b, place, deg)
                v.engine_nop().then_inc(s["ct"], 1)
                pick(key, iota_b, place, iota_b)
                v.tensor_scalar(order[g.name][:, :], key[:, :], float(P), lane_f[:, 0:1], ALU.mult, ALU.add)
                v.wait_ge(s["cp"], 2)
                v.tensor_reduce(ng[:, :], bank[3][0:NB, 0:P], AX.X, ALU.max)
                v.drain()
                v.tensor_scalar(ngi[:, :], ng[:, :], 1.0, float(UNIT - 1), ALU.max, ALU.add)
                v.drain()
                v.tensor_scalar(ngi[:, :], ngi[:, :], UNIT_LOG, None, ALU.logical_shift_right)
                v.drain()
                v.tensor_copy(ng[:, :], ngi[:, :])
                v.drain()
                v.tensor_scalar(ngr[:, :], bc(ng[:, :], [NB, P]), float(UNIT), None, ALU.mult)
                v.drain().then_inc(s["ct"], 1)
                v.wait_ge(s["cp"], 3)
                v.tensor_copy(sdeg[:, :], bank[3][:, 0:NB])
                c = cum[g.name]
                v.tensor_copy(c[:, 0:NB + 1], bank[2][0:1, 0:NB + 1])
                v.drain()
                v.tensor_scalar(c[:, NB:NB + 1], c[:, NB:NB + 1], float(MIN_UNITS), float(RING - 1), ALU.max, ALU.add)
                v.drain()
                v.tensor_scalar(c[:, NB:NB + 1], c[:, NB:NB + 1], RING_LOG, RING_LOG, ALU.logical_shift_right, ALU.logical_shift_left)
                v.drain()
                v.tensor_scalar(c[:, NB + 1:NB + 2], c[:, NB:NB + 1], 1.0 / RING, -1.0, ALU.mult, ALU.add)
                v.drain()
                v.tensor_scalar(c[:, NB + 2:NB + 3], c[:, NB:NB + 1], float(FILL * g.filled), 0.0, ALU.subtract, ALU.max)
                v.drain()
                v.tensor_scalar(c[:, NB + 2:NB + 3], c[:, NB + 2:NB + 3], float(2 * FILL - 1), None, ALU.add)
                v.drain()
                v.tensor_scalar(c[:, NB + 2:NB + 3], c[:, NB + 2:NB + 3], FILL_LOG, None, ALU.logical_shift_right)
                begins = unit_begins[g.name]
                v.tensor_tensor(begins, bc(unit_round[:, :].unsqueeze(2), [P, UK, NB - 1]), bc(sdeg[:, 1:NB].unsqueeze(1), [P, UK, NB - 1]), ALU.is_ge)
                v.drain()
                v.tensor_reduce(block_sum, begins, AX.X, ALU.add)
                v.drain()
                v.tensor_copy(block_of_unit, block_sum)
                v.drain().then_inc(s["cumw"], 1)
                pick(seed, place, iota_b, sdeg)
                v.engine_nop().then_inc(s["seedin"], 1)

            def ranks(g):
                s = st[g.name]
                v.engine_nop().then_inc(s["ranked"], 2)

                def first_half(n, o):
                    onehots(n, o).then_inc(s["oh2"], 1)

                def pairs(n, h):
                    v.wait_ge(s["fr"], n + 1)
                    return v.tensor_tensor(Tm[:, h], bank[4 + h][:, :].rearrange("p (k e) -> p k e", k=BATCH),
                                           bc(hi_b[:, bass.ds(n * BATCH, BATCH)].unsqueeze(2), [P, BATCH, P]), ALU.is_equal).then_inc(s["tm"], 1)

                def look_up(n, o, h):
                    v.wait_ge(s["gr"], n + 1)
                    for k in range(BATCH):
                        m = v.scalar_tensor_tensor(out=junk[:, k, :], in0=bank[2 + h][:, k * P:(k + 1) * P], scalar=1.0,
                                                   in1=OL[:, o, k, :], op0=ALU.mult, op1=ALU.mult, accum_out=rank[:, k:k + 1])
                    m.then_inc(s["ranked"], 1)

                def slots(n, h, use):
                    v.drain()
                    v.tensor_copy(rank_i[:, :], rank[:, :])
                    v.drain()
                    if not isinstance(use, int) or use > 0:
                        v.wait_ge(s["sc"][h], use * (16 * BATCH))
                    v.tensor_scalar(q_i[:, :], rank_i[:, :], UNIT_LOG, UNIT_LOG + 7, ALU.logical_shift_right, ALU.logical_shift_left)
                    v.scalar_tensor_tensor(out=b_i[:, :], in0=rank_i[:, :], scalar=UNIT - 1,
                                           in1=lane_slot[:, bass.ds(n * BATCH, BATCH)], op0=ALU.bitwise_and, op1=ALU.bitwise_or)
                    v.tensor_copy(load[:, h, :], src_i[:, bass.ds(n * BATCH, BATCH)])
                    v.drain()
                    v.tensor_tensor(addr[:, h, :], q_i[:, :].bitcast(U32), b_i[:, :].bitcast(U32), ALU.bitwise_or).then_inc(s["ad"], 1)

                last = g.batches // OHS - 1

                def step(i, j, project):
                    n = OHS * i + j
                    end = isinstance(i, int) and i == last
                    if project and j == 0:
                        normalise(g, i)
                    if not end or j == 0:
                        first_half(n + 3, (j + 3) % OHS)
                    look_up(n, j, j % 2)
                    slots(n, j, i)
                    if not end or j < 2:
                        pairs(n + 2, j % 2)
                    if project and j == 3:
                        projected(g, i)

                for n in range(3):
                    first_half(n, n)
                    if n > 0:
                        pairs(n - 1, n - 1)
                rank_steps(g, v, step)

            def attend(g, on_pe, per_block=None, lag=0):
                s = st[g.name]
                H, C, HC = g.heads, g.width, g.hc
                a, m = accs[g.name], mrun[g.name]
                z = zt[:, :, 0:H]
                if on_pe:
                    v.sem_inc(s["ps"], 2)
                    v.sem_inc(s["pa"], 2)

                def slot_block(of, h):
                    v.sem_inc(s_vstep, 1)
                    return v.value_load(of[0:1, h:h + 1], min_val=0, max_val=NB - 1)

                def logits(q, h):
                    rows = ring[g.name][h]
                    e_ = ed[:, h % 2, 0:UNIT * H].rearrange("p (r h) -> p r h", r=UNIT)
                    old = ed[:, h % 2, UNIT * H:(UNIT + 1) * H]
                    v.wait_ge(s["ga"][h], (q + 1) * (16 * UNIT))
                    b = slot_block(ub, h)
                    v.tensor_copy(ub_own[:, h:h + 1], ub[:, h:h + 1])
                    v.tensor_tensor(z, rows[:, :, HC:HC + H], bc(blk(a, b, HC + H, HC + 2 * H).unsqueeze(1), [P, UNIT, H]), ALU.add)
                    v.drain()
                    v.scalar_tensor_tensor(out=e_, in0=z, scalar=SLOPE, in1=z, op0=ALU.mult, op1=ALU.max)
                    v.drain()
                    v.tensor_reduce(gm[:, 0:H], e_.rearrange("p r h -> p h r"), AX.X, ALU.max)
                    v.drain()
                    v.tensor_tensor(mnew[:, 0:H], gm[:, 0:H], blk(m, b), ALU.max)
                    v.drain()
                    v.tensor_tensor(e_, e_, bc(mnew[:, 0:H].unsqueeze(1), [P, UNIT, H]), ALU.subtract)
                    v.tensor_tensor(old, blk(m, b), mnew[:, 0:H], ALU.subtract).then_inc(s["ed"], 1)
                    v.drain()
                    v.tensor_copy(blk(m, b), mnew[:, 0:H]).then_inc(s["noted"], 1)

                def products(q, h):
                    u = RING * q + h
                    w_ = wt[:, h % 2, 0:UNIT * H].rearrange("p (r h) -> p r h", r=UNIT)
                    v.wait_ge(s["w"], u + 1)
                    if on_pe:
                        v.wait_ge(s["ps"], u + 1)
                    p_ = v.tensor_tensor(prod[g.name][h % 2].rearrange("p r (h c) -> p r h c", c=C),
                                         ring[g.name][h][:, :, 0:HC].rearrange("p r (h c) -> p r h c", c=C),
                                         bc(w_.unsqueeze(3), [P, UNIT, H, C]), ALU.mult)
                    if on_pe:
                        p_.then_inc(s["pr"], 1)
                    v.tensor_reduce(den_p[:, h % 2, 0:H], w_.rearrange("p r h -> p h r"), AX.X, ALU.add).then_inc(s["ru"], 1)

                def add_sums(u, h):
                    sc_ = wt[:, h % 2, UNIT * H:(UNIT + 1) * H]
                    b = slot_block(ub_own, h)
                    total, sums = blk(a, b, HC, HC + H), blk(a, b, 0, HC)
                    v.tensor_tensor(sums.rearrange("p (h c) -> p h c", c=C), sums.rearrange("p (h c) -> p h c", c=C),
                                    bc(sc_.unsqueeze(2), [P, H, C]), ALU.mult)
                    v.tensor_tensor(total, total, sc_, ALU.mult)
                    if not on_pe:
                        v.tensor_reduce(part_f[:, 0:HC], prod[g.name][h % 2].rearrange("p r w -> p w r"), AX.X, ALU.add)
                    v.drain()
                    v.tensor_tensor(total, total, den_p[:, h % 2, 0:H], ALU.add)
                    if on_pe:
                        v.wait_ge(s["ps"], u + 3)
                        v.tensor_tensor(sums, sums, bank[4 + h % 2][:, 0:HC], ALU.add).then_inc(s["pa"], 1)
                    else:
                        v.tensor_tensor(sums, sums, part_f[:, 0:HC], ALU.add)
                    v.drain()

                def half_quad(q, half, last):
                    for h in (2 * half, 2 * half + 1):
                        products(q, h)
                        if h > 0 or not isinstance(q, int) or q > 0:
                            add_sums(RING * q + h - 1, (h - 1) % RING)
                        if not last or h < RING - 1:
                            logits(q + (h + 1) // RING, (h + 1) % RING)
                            v.drain()

                logits(0, 0)
                v.drain()
                last = quads_of(g, v, half_quad, per_block, lag)
                add_sums(RING * last + RING - 1, RING - 1)

            for g in (GNN, FFN):
                v.sem_inc(st[g.name]["hist"], 1)
            split_edges(GNN)
            for j in range(2 * OHS):
                histogram(GNN, j, j)
            with v.Fori(2, GNN.batches // OHS) as i:
                for j in range(OHS):
                    histogram(GNN, OHS * i + j, OHS + j)
            order_nodes(GNN)

            v.wait_ge(s_xin, 32)
            with v.Fori(0, NB // 7) as i:
                for j in range(7):
                    mean_var(blk(xn_all, i * 7 + j), i * 7 + j)
            v.drain()
            for b in range(NB):
                v.bn_aggr(mv[:, b, :], stats[:, b, :])
            v.drain().then_inc(s_var, 1)
            v.wait_ge(s_sd, 1)
            v.reciprocal(rstd[:, :], rstd[:, :])
            v.drain()
            ranks(GNN)
            v.wait_ge(s_norm, 16 * 6)
            state(GNN)
            for h in range(OHS):
                v.wait_ge(st["gnn"]["sc"][h], 16 * BATCH * (GNN.batches // OHS))
            split_edges(FFN)

            def next_histogram(b):
                for j in range(HPB):
                    histogram(FFN, b * HPB + j, j)

            attend(GNN, True, next_histogram)
            for j in range(FFN.batches - NB * HPB):
                histogram(FFN, NB * HPB + j, j)
            order_nodes(FFN)

            v.drain().then_inc(st["gnn"]["end"], 1)
            with v.Fori(0, NC) as c:
                o = acc[:, bass.ds(c * CH, CH), 0:D]
                dn = acc[:, bass.ds(c * CH, CH), D:D + GNN.heads]
                o4 = o.rearrange("p b (h c) -> p b h c", h=GNN.heads)
                v.tensor_scalar(dn, dn, 1e-16, None, ALU.add)
                v.drain()
                v.reciprocal(dn, dn)
                v.drain()
                v.tensor_tensor(o4, o4, bc(dn.unsqueeze(3), [P, CH, GNN.heads, GNN.width]), ALU.mult)
                v.drain()
                v.tensor_tensor(o, o, bc(par[:, 0:1, :], [P, CH, D]), ALU.add)
                v.drain()
                for j in range(CH):
                    v.bn_stats(stats[:, j, :], blk(acc, c * CH + j, 0, D))
                v.drain()
                for j in range(CH):
                    a_ = v.bn_aggr(mv[:, j, :], stats[:, j, :])
                a_.then_inc(s_sdo, 1)
                v.wait_ge(s_sdo2, c + 1)
                v.reciprocal(rstd[:, 0:CH], rstd[:, 0:CH])
                v.drain()
                for j in range(CH):
                    ob = blk(acc, c * CH + j, 0, D)
                    v.tensor_scalar(ob, ob, mv[:, j, 0:1], rstd[:, j:j + 1], ALU.subtract, ALU.mult)
                v.drain()
                v.tensor_tensor(o, o, bc(par[:, 1:2, :], [P, CH, D]), ALU.mult)
                v.drain()
                v.tensor_tensor(o, o, bc(par[:, 2:3, :], [P, CH, D]), ALU.add)
                v.drain().then_inc(st["gnn"]["fin"], 1)

            v.wait_ge(s_x2, 32)
            v.wait_ge(st["gnn"]["back"], 16)
            with v.Fori(0, NC) as c:
                o = acc[:, bass.ds(c * CH, CH), 0:D]
                v.tensor_tensor(o, o, xn_all[:, bass.ds(c * CH, CH), :], ALU.add)
                v.drain()
                for j in range(CH):
                    v.bn_stats(stats[:, j, :], blk(acc, c * CH + j, 0, D))
                v.drain()
                for j in range(CH):
                    v.bn_aggr(mv[:, j, :], stats[:, j, :])
                v.drain()
                v.tensor_copy(mv2[:, bass.ds(c * CH, CH), :], mv[:, 0:CH, :])
                v.drain()
            v.drain().then_inc(s_var, 1)
            v.wait_ge(s_sd, 2)
            v.reciprocal(rstd[:, :], rstd[:, :])
            v.drain()

            ranks(FFN)
            state(FFN)
            for h in range(OHS):
                v.wait_ge(st["ffn"]["sc"][h], 16 * BATCH * (FFN.batches // OHS))
            v.sem_inc(s_ys, 16)
            v.sem_inc(s_yu, NE)
            v.wait_ge(s_par, 16 * (3 * NE + 1))

            def expert_outputs(b):
                v.wait_ge(s_ys, b * 16 + 16)
                for e in range(NE):
                    v.wait_ge(s_y, b * NE + e + NE + 1)
                    m = v.tensor_tensor(y[:, e, :], bank[2 + e][:, 0:D], b2b[:, e, :], ALU.add)
                    m.then_inc(s_yu, 1)
                v.drain().then_inc(s_yr, 1)

            attend(FFN, False, expert_outputs, lag=1)

            fo = facc[:, :, 0:16]
            fd = facc[:, :, 16:16 + FHEADS]
            v.tensor_scalar(fd, fd, 1e-16, None, ALU.add)
            v.drain()
            v.reciprocal(fd, fd)
            v.drain()
            v.tensor_tensor(fo.rearrange("p b (h c) -> p b h c", h=FHEADS), fo.rearrange("p b (h c) -> p b h c", h=FHEADS),
                            bc(fd.unsqueeze(3), [P, NB, FHEADS, NE]), ALU.mult)
            v.drain().then_inc(st["ffn"]["fin"], NC)
            v.wait_ge(st["ffn"]["back"], 16)
            v.tensor_tensor(fo, fo, bc(fpar[:, 0:1, :], [P, NB, 16]), ALU.add)
            v.drain()
            v.tensor_reduce(mv2[:, :, 0], fo, AX.X, ALU.add)
            v.drain()
            v.tensor_scalar(mv2[:, :, 0], mv2[:, :, 0], 1.0 / 16, None, ALU.mult)
            v.drain()
            v.tensor_tensor(fo, fo, bc(mv2[:, :, 0:1], [P, NB, 16]), ALU.subtract)
            v.drain()
            v.tensor_tensor(lnf[:, :, :], fo, fo, ALU.mult)
            v.drain()
            v.tensor_reduce(mv2[:, :, 1], lnf[:, :, :], AX.X, ALU.add)
            v.drain()
            v.tensor_scalar(mv2[:, :, 1], mv2[:, :, 1], 1.0 / 16, None, ALU.mult)
            v.drain().then_inc(s_zf, 1)
            v.wait_ge(s_zf2, 1)
            v.reciprocal(rstd[:, :], rstd[:, :])
            v.drain()
            v.tensor_tensor(fo, fo, bc(rstd[:, :].unsqueeze(2), [P, NB, 16]), ALU.mult)
            v.drain()
            v.tensor_tensor(fo, fo, bc(fpar[:, 1:2, :], [P, NB, 16]), ALU.mult)
            v.drain()
            v.tensor_tensor(fo, fo, bc(fpar[:, 2:3, :], [P, NB, 16]), ALU.add)
            v.drain()
            v.tensor_reduce(sc[:, :, :], fo.rearrange("p b (h e) -> p b e h", h=FHEADS), AX.X, ALU.add)
            v.drain()
            v.tensor_scalar(sc[:, :, :], sc[:, :, :], 1.0 / FHEADS, None, ALU.mult)
            v.memset(cnt[:, :, :], 0.0)
            v.drain()
            for e in range(NE):
                for o in range(NE):
                    if o != e:
                        v.tensor_tensor(cmp[:, :], sc[:, :, o], sc[:, :, e], ALU.is_ge if o < e else ALU.is_gt)
                        v.drain()
                        v.tensor_tensor(cnt[:, :, e], cnt[:, :, e], cmp[:, :], ALU.add)
                        v.drain()
            v.tensor_reduce(cmp[:, :], sc[:, :, :], AX.X, ALU.max)
            v.drain()
            v.tensor_tensor(sc[:, :, :], sc[:, :, :], bc(cmp[:, :].unsqueeze(2), [P, NB, NE]), ALU.subtract)
            v.tensor_scalar(cnt[:, :, :], cnt[:, :, :], 1.5, None, ALU.is_lt)
            v.drain().then_inc(s_zf, 1)
            v.wait_ge(s_zf2, 2)
            v.tensor_tensor(gate[:, :, :], gate[:, :, :], cnt[:, :, :], ALU.mult)
            v.drain()
            v.tensor_reduce(cmp[:, :], gate[:, :, :], AX.X, ALU.add)
            v.drain()
            v.reciprocal(cmp[:, :], cmp[:, :])
            v.drain()
            v.tensor_tensor(gate[:, :, :], gate[:, :, :], bc(cmp[:, :].unsqueeze(2), [P, NB, NE]), ALU.mult)
            v.drain().then_inc(s_gate, 1)

            with v.Fori(0, NC) as c:
                for j in range(CH):
                    v.wait_ge(s_yb[j], (c + 1) * 16)
                    for e in range(NE):
                        o = blk(acc, c * CH + j, 0, D)
                        gt = gate[:, bass.ds(c * CH + j, 1), e]
                        m = v.scalar_tensor_tensor(out=o, in0=yback[:, j, e, :], scalar=gt, in1=o, op0=ALU.mult, op1=ALU.add)
                        if e == NE - 1:
                            m.then_inc(s_yfree, 1)
                        v.drain()
                v.engine_nop().then_inc(s_fin, 1)


_INS = ["x", "src", "dst", "L0_gnn_W", "L0_gnn_att_src", "L0_gnn_att_dst", "L0_gnn_bias", "L0_gnn_ln_gamma",
        "L0_gnn_ln_beta", "L0_ffn_W_gat", "L0_ffn_att_src", "L0_ffn_att_dst", "L0_ffn_b_gat", "L0_ffn_ln_gamma",
        "L0_ffn_ln_beta", "L0_ffn_W1", "L0_ffn_b1", "L0_ffn_W2", "L0_ffn_b2", "L0_ffn_edge_index"]


def kernel(**inputs):
    import concourse.bacc as bacc
    from concourse.bass_utils import run_bass_kernel_spmd

    nc = bacc.Bacc("TRN2", target_bir_lowering=False, num_devices=1)
    arrays, args = {}, []
    for name in _INS:
        a = np.ascontiguousarray(inputs[name])
        arrays[f"in_{name}"] = a
        args.append(nc.dram_tensor(f"in_{name}", a.shape, mybir.dt.from_np(a.dtype), kind="ExternalInput").ap())
    args.append(nc.dram_tensor("out", (N, D), F32, kind="ExternalOutput").ap())
    build(nc, *args)
    r = run_bass_kernel_spmd(nc, [arrays], core_ids=[0])
    return r.results[0]["out"]
```
